# Optimizing a Trainium2 kernel written in Bass

```python
import numpy as np
import jax
import jax.numpy as jnp

def _softmax(x, axis=-1):
    return jax.nn.softmax(x, axis=axis)

def _gelu(x):
    return jax.nn.gelu(x, approximate=True)

def _silu(x):
    return jax.nn.silu(x)

def _sigmoid(x):
    return jax.nn.sigmoid(x)

def _layernorm(x, axis=-1, eps=1e-05):
    m = jnp.mean(x, axis=axis, keepdims=True)
    v = jnp.var(x, axis=axis, keepdims=True)
    return (x - m) / jnp.sqrt(v + eps)

def _scatter_add(tgt, idx, src, axis=0):
    return tgt.at[idx].add(src)

def _segment_sum(src, seg, n):
    return jax.ops.segment_sum(src, seg, n)
kernel_name = 'mk_decoder_postln_d4_seqx_r4_1b52d3'

def setup_inputs(seed: int=0):
    np.random.seed(seed)
    _w = jnp.asarray

    def _rec_inputs():
        import jax
        import jax.numpy as jnp
        _rk = jax.random.key(seed)
        x = 7.22e-05 + 1 * jax.random.normal(jax.random.fold_in(_rk, 1), (16, 128, 256), jnp.float32)
        _lenS = 128 - jax.random.randint(jax.random.fold_in(_rk, 7), (16,), 0, max(1, 128 // 4) + 1, jnp.int32)
        _lenS2 = 128 - jax.random.randint(jax.random.fold_in(_rk, 8), (16,), 0, max(1, 128 // 4) + 1, jnp.int32)
        _ctx_1024P = jax.random.normal(jax.random.fold_in(_rk, 11), (16, 16, 256), jnp.float32)
        _ctx_1024c = jax.random.dirichlet(jax.random.fold_in(_rk, 511), 0.3 * jnp.ones((16,), jnp.float32), (16, 128))
        _ctx_1024t = jnp.einsum('bsk,bkd->bsd', _ctx_1024c, _ctx_1024P)
        _ctx_1024t = _ctx_1024t * jax.lax.rsqrt(jnp.mean(jnp.square(_ctx_1024t)) + 1e-12) * 0.953939
        ctx_1024 = -1.39393e-06 + 0.999914 * (_ctx_1024t + 0.3 * jax.random.normal(jax.random.fold_in(_rk, 611), (16, 128, 256), jnp.float32))
        _validS = jnp.arange(128)[None, :] < _lenS[:, None]
        _validS2 = jnp.arange(128)[None, :] < _lenS2[:, None]
        _causal = jnp.tril(jnp.ones((128, 128), dtype=bool))
        mask_BxSxS2_if1 = jnp.where(jnp.ones((16, 128, 128), dtype=bool), 1, 0).astype(jnp.int32)
        return (x, ctx_1024, mask_BxSxS2_if1)
    x, ctx_1024, mask_BxSxS2_if1 = _rec_inputs()

    def _L0_attn_setup():
        import jax, jax.numpy as jnp
        import numpy as np
        B_SZ, T, D_IN, H = (8, 256, 256, 256)
        key = jax.random.key(seed)
        ks = jax.random.split(key, 9)
        lim_u = 1.0 / np.sqrt(D_IN)
        return {'x': jax.random.normal(ks[0], (B_SZ, T, D_IN), dtype=jnp.float32), 'W_u': jax.random.uniform(ks[1], (H, D_IN), jnp.float32, -lim_u, lim_u), 'b_u': jax.random.uniform(ks[2], (H,), jnp.float32, -lim_u, lim_u), 'W_g': jax.random.uniform(ks[3], (H, D_IN), jnp.float32, -lim_u, lim_u), 'b_g': jax.random.uniform(ks[4], (H,), jnp.float32, -lim_u, lim_u), 'A': jnp.eye(H, dtype=jnp.float32) * 0.6, 'Bm': jax.random.normal(ks[5], (H, H), dtype=jnp.float32), 'Cm': jax.random.normal(ks[6], (H, H), dtype=jnp.float32), 'D': jax.random.normal(ks[7], (H,), dtype=jnp.float32)}
    _L0_attn_all = _L0_attn_setup()
    _L0_attn_in = {k: v for k, v in _L0_attn_all.items() if k in ('W_u', 'b_u', 'W_g', 'b_g', 'A', 'Bm', 'Cm', 'D')}
    del _L0_attn_all

    def _L0_xattn_setup():
        import jax, jax.numpy as jnp
        import numpy as np
        EPS = 1e-05

        def layernorm(x, g, b):
            mu = jnp.mean(x, axis=-1, keepdims=True)
            var = jnp.var(x, axis=-1, keepdims=True)
            return (x - mu) * jax.lax.rsqrt(var + EPS) * g + b
        DIM = 256
        CTX = 256
        HEADS = 12
        DHEAD = 64
        INNER = HEADS * DHEAD
        B = 4
        F = 512
        J = 256
        key = jax.random.key(seed)
        ks = jax.random.split(key, 8)
        s = lambda d: 1.0 / np.sqrt(d)
        return {'x': jax.random.normal(ks[0], (B, F, DIM), jnp.float32), 'tab_x': jax.random.normal(ks[1], (B, J, CTX), jnp.float32), 'tab_g': jnp.ones((CTX,), jnp.float32), 'tab_b': jnp.zeros((CTX,), jnp.float32), 'vid_g': jnp.ones((DIM,), jnp.float32), 'vid_b': jnp.zeros((DIM,), jnp.float32), 'Wq': jax.random.normal(ks[2], (DIM, INNER), jnp.float32) * s(DIM), 'Wk': jax.random.normal(ks[3], (CTX, INNER), jnp.float32) * s(CTX), 'Wv': jax.random.normal(ks[4], (CTX, INNER), jnp.float32) * s(CTX), 'q_g': jnp.ones((INNER,), jnp.float32), 'q_b': jnp.zeros((INNER,), jnp.float32), 'k_g': jnp.ones((INNER,), jnp.float32), 'k_b': jnp.zeros((INNER,), jnp.float32), 'Wo': jax.random.normal(ks[5], (INNER, DIM), jnp.float32) * s(INNER), 'bo': jnp.zeros((DIM,), jnp.float32)}
    _L0_xattn_all = _L0_xattn_setup()
    _L0_xattn_in = {k: v for k, v in _L0_xattn_all.items() if k in ('tab_g', 'tab_b', 'vid_g', 'vid_b', 'Wq', 'Wk', 'Wv', 'q_g', 'q_b', 'k_g', 'k_b', 'Wo', 'bo')}
    del _L0_xattn_all

    def _L0_ffn_setup():
        import jax, jax.numpy as jnp
        import numpy as np
        HIDDEN = 256
        INNER = 1024

        def _weight_quant(w):
            scale = 1.0 / jnp.clip(jnp.mean(jnp.abs(w)), 1e-05)
            wq = jnp.clip(jnp.round(w * scale), -1.0, 1.0) / scale
            return w + jax.lax.stop_gradient(wq - w)

        def _act_quant(x):
            scale = 127.0 / jnp.clip(jnp.max(jnp.abs(x), axis=-1, keepdims=True), 1e-05)
            xq = jnp.clip(jnp.round(x * scale), -128.0, 127.0) / scale
            return x + jax.lax.stop_gradient(xq - x)

        def _bitlinear(x, w):
            return jnp.einsum('bsi,oi->bso', _act_quant(x), _weight_quant(w))
        key = jax.random.key(seed)
        k0, k1, k2, k3 = jax.random.split(key, 4)
        x = jax.random.normal(k0, (4, 512, HIDDEN), dtype=jnp.float32)
        w_gate = jax.random.normal(k1, (INNER, HIDDEN), dtype=jnp.float32) / np.sqrt(HIDDEN)
        w_up = jax.random.normal(k2, (INNER, HIDDEN), dtype=jnp.float32) / np.sqrt(HIDDEN)
        w_down = jax.random.normal(k3, (HIDDEN, INNER), dtype=jnp.float32) / np.sqrt(INNER)
        return {'x': x, 'w_gate': w_gate, 'w_up': w_up, 'w_down': w_down}
    _L0_ffn_all = _L0_ffn_setup()
    _L0_ffn_in = {k: v for k, v in _L0_ffn_all.items() if k in ('w_gate', 'w_up', 'w_down')}
    del _L0_ffn_all

    def _L1_attn_setup():
        import jax, jax.numpy as jnp
        import numpy as np
        D_MODEL, D_STATE, D_INNER = (256, 16, 512)
        EPS = 1e-05

        def bit_linear(x, w, b):
            scale = jnp.maximum(jnp.mean(jnp.abs(w)), EPS)
            ws = w / scale
            wq = ws + jax.lax.stop_gradient(jnp.clip(jnp.round(ws), -1.0, 1.0) - ws)
            return jnp.einsum('bsd,od->bso', x, wq) * scale + b

        def causal_dwconv(x, w, b):
            xc = jnp.transpose(x, (0, 2, 1))
            y = jax.lax.conv_general_dilated(xc, w, window_strides=(1,), padding=[(3, 0)], feature_group_count=w.shape[0], dimension_numbers=('NCH', 'OIH', 'NCH'))
            y = y + b[None, :, None]
            return jnp.transpose(y, (0, 2, 1))
        key = jax.random.key(seed)
        ks = jax.random.split(key, 9)
        B, S = (4, 1024)
        return {'x': jax.random.normal(ks[0], (B, S, D_MODEL), dtype=jnp.float32), 'w_in': jax.random.normal(ks[1], (2 * D_INNER, D_MODEL), dtype=jnp.float32) * 0.02, 'b_in': jax.random.normal(ks[2], (2 * D_INNER,), dtype=jnp.float32) * 0.02, 'w_conv': jax.random.normal(ks[3], (D_INNER, 1, 4), dtype=jnp.float32) * 0.2, 'b_conv': jax.random.normal(ks[4], (D_INNER,), dtype=jnp.float32) * 0.02, 'w_x': jax.random.normal(ks[5], (D_STATE + D_MODEL + D_INNER, D_INNER), dtype=jnp.float32) * 0.02, 'b_x': jax.random.normal(ks[6], (D_STATE + D_MODEL + D_INNER,), dtype=jnp.float32) * 0.02, 'w_out': jax.random.normal(ks[7], (D_MODEL, D_INNER), dtype=jnp.float32) * 0.02, 'b_out': jax.random.normal(ks[8], (D_MODEL,), dtype=jnp.float32) * 0.02}
    _L1_attn_all = _L1_attn_setup()
    _L1_attn_in = {k: v for k, v in _L1_attn_all.items() if k in ('w_in', 'b_in', 'w_conv', 'b_conv', 'w_x', 'b_x', 'w_out', 'b_out')}
    del _L1_attn_all

    def _L1_xattn_setup():
        import jax, jax.numpy as jnp
        import numpy as np
        DIM = 256
        N_HEADS = 16
        HEAD_DIM = DIM // N_HEADS
        GAMMA = 10.0

        def larope_cos_sin(seq_len, gamma, head_dim):
            inv_freq = 1.0 / 10000.0 ** (jnp.arange(0, head_dim, 2, dtype=jnp.float32) / head_dim)
            t = jnp.arange(seq_len, dtype=jnp.float32)
            freqs = jnp.outer(gamma * (t / seq_len), inv_freq)
            emb = jnp.concatenate([freqs, freqs], axis=-1)
            return (jnp.cos(emb), jnp.sin(emb))

        def apply_rope(x, cos, sin):
            d = x.shape[-1] // 2
            x1, x2 = (x[..., :d], x[..., d:])
            c = cos[None, None, :, :d]
            s = sin[None, None, :, :d]
            return jnp.concatenate([x1 * c - x2 * s, x1 * s + x2 * c], axis=-1)
        key = jax.random.key(seed)
        ks = jax.random.split(key, 11)
        B, Lq, Lk = (4, 512, 256)
        std = 1.0 / np.sqrt(DIM)
        inp = {'query': jax.random.normal(ks[0], (B, Lq, DIM), dtype=jnp.float32), 'key': jax.random.normal(ks[1], (B, Lk, DIM), dtype=jnp.float32), 'value': jax.random.normal(ks[2], (B, Lk, DIM), dtype=jnp.float32), 'Wq': jax.random.normal(ks[3], (DIM, DIM), dtype=jnp.float32) * std, 'bq': jnp.zeros((DIM,), dtype=jnp.float32), 'Wk': jax.random.normal(ks[4], (DIM, DIM), dtype=jnp.float32) * std, 'bk': jnp.zeros((DIM,), dtype=jnp.float32), 'Wv': jax.random.normal(ks[5], (DIM, DIM), dtype=jnp.float32) * std, 'bv': jnp.zeros((DIM,), dtype=jnp.float32), 'Wo': jax.random.normal(ks[6], (DIM, DIM), dtype=jnp.float32) * std, 'bo': jnp.zeros((DIM,), dtype=jnp.float32)}
        return inp
    _L1_xattn_all = _L1_xattn_setup()
    _L1_xattn_in = {k: v for k, v in _L1_xattn_all.items() if k in ('Wq', 'bq', 'Wk', 'bk', 'Wv', 'bv', 'Wo', 'bo')}
    del _L1_xattn_all

    def _L1_ffn_setup():
        import jax, jax.numpy as jnp
        import numpy as np
        DIM = 256
        HID = 1024
        E = 8
        TOPK = 2
        ALPHA = 2.0
        B, T = (1, 512)
        DOWN_SCALE = 0.01
        key = jax.random.key(seed)
        ks = jax.random.split(key, 8)
        s = 1.0 / np.sqrt(DIM)
        sh = 1.0 / np.sqrt(HID)
        return {'x': jax.random.normal(ks[0], (B, T, DIM), jnp.float32), 'w_router': jax.random.uniform(ks[1], (DIM, E), jnp.float32, -s, s), 'w_up': jax.random.uniform(ks[2], (E - 1, DIM, HID), jnp.float32, -s, s), 'w_gate': jax.random.uniform(ks[3], (E - 1, DIM, HID), jnp.float32, -s, s), 'w_down': jax.random.normal(ks[4], (E - 1, HID, DIM), jnp.float32) * DOWN_SCALE, 'ws_up': jax.random.uniform(ks[5], (DIM, HID), jnp.float32, -s, s), 'ws_gate': jax.random.uniform(ks[6], (DIM, HID), jnp.float32, -s, s), 'ws_down': jax.random.normal(ks[7], (HID, DIM), jnp.float32) * DOWN_SCALE}
    _L1_ffn_all = _L1_ffn_setup()
    _L1_ffn_in = {k: v for k, v in _L1_ffn_all.items() if k in ('w_router', 'w_up', 'w_gate', 'w_down', 'ws_up', 'ws_gate', 'ws_down')}
    del _L1_ffn_all

    def _L2_attn_setup():
        import jax, jax.numpy as jnp
        import numpy as np
        B, T, E = (4, 512, 256)
        H, D = (8, 128)

        def sinusoidal_pe(length, dim, dtype=jnp.float32):
            pos = jnp.arange(length, dtype=jnp.float32)[:, None]
            inv_freq = jnp.exp(-jnp.log(jnp.float32(10000.0)) * (jnp.arange(0, dim, 2, dtype=jnp.float32) / dim))
            ang = pos * inv_freq[None, :]
            pe = jnp.zeros((length, dim), dtype=jnp.float32)
            pe = pe.at[:, 0::2].set(jnp.sin(ang)).at[:, 1::2].set(jnp.cos(ang))
            return pe.astype(dtype)
        key = jax.random.key(seed)
        kx, kq, kk, kv, ko = jax.random.split(key, 5)
        s = 0.02
        return {'x': jax.random.normal(kx, (B, T, E), dtype=jnp.float32), 'Wq': jax.random.normal(kq, (H * D, E), dtype=jnp.float32) * s, 'Wk': jax.random.normal(kk, (D, E), dtype=jnp.float32) * s, 'Wv': jax.random.normal(kv, (D, E), dtype=jnp.float32) * s, 'Wo': jax.random.normal(ko, (E, H * D), dtype=jnp.float32) * s}
    _L2_attn_all = _L2_attn_setup()
    _L2_attn_in = {k: v for k, v in _L2_attn_all.items() if k in ('Wq', 'Wk', 'Wv', 'Wo')}
    del _L2_attn_all

    def _L2_xattn_setup():
        import jax, jax.numpy as jnp
        import numpy as np
        D_MODEL = 256
        HEADS = 16
        D_K = D_MODEL // HEADS
        key = jax.random.key(seed)
        ks = jax.random.split(key, 8)
        B, S = (2, 512)
        scale = 1.0 / np.sqrt(D_MODEL)
        return {'q': jax.random.normal(ks[0], (B, S, D_MODEL), dtype=jnp.float32), 'k': jax.random.normal(ks[1], (B, S, D_MODEL), dtype=jnp.float32), 'v': jax.random.normal(ks[2], (B, S, D_MODEL), dtype=jnp.float32), 'mask': jnp.ones((B, S, S), dtype=jnp.int32), 'w_q': jax.random.normal(ks[3], (D_MODEL, D_MODEL), dtype=jnp.float32) * scale, 'w_k': jax.random.normal(ks[4], (D_MODEL, D_MODEL), dtype=jnp.float32) * scale, 'w_v': jax.random.normal(ks[5], (D_MODEL, D_MODEL), dtype=jnp.float32) * scale, 'w_o': jax.random.normal(ks[6], (D_MODEL, D_MODEL), dtype=jnp.float32) * scale, 'b_o': jnp.zeros((D_MODEL,), dtype=jnp.float32)}
    _L2_xattn_all = _L2_xattn_setup()
    _L2_xattn_in = {k: v for k, v in _L2_xattn_all.items() if k in ('w_q', 'w_k', 'w_v', 'w_o', 'b_o')}
    del _L2_xattn_all

    def _L2_ffn_setup():
        import jax, jax.numpy as jnp
        import numpy as np
        CAPACITY_FACTOR = 1.0
        key = jax.random.key(seed)
        ks = jax.random.split(key, 5)
        B, S, D, E, F = (2, 512, 256, 8, 1024)
        x = jax.random.normal(ks[0], (B, S, D), dtype=jnp.float32)
        Ws = jax.random.normal(ks[1], (D, E), dtype=jnp.float32) * (1.0 / np.sqrt(D))
        bs = jnp.zeros((E,), dtype=jnp.float32)
        W1 = jax.random.normal(ks[2], (E, D, F), dtype=jnp.float32) * (1.0 / np.sqrt(D))
        b1 = jnp.zeros((E, F), dtype=jnp.float32)
        W2 = jax.random.normal(ks[3], (E, F, D), dtype=jnp.float32) * (1.0 / np.sqrt(F))
        b2 = jnp.zeros((E, D), dtype=jnp.float32)
        return {'x': x, 'Ws': Ws, 'bs': bs, 'W1': W1, 'b1': b1, 'W2': W2, 'b2': b2}
    _L2_ffn_all = _L2_ffn_setup()
    _L2_ffn_in = {k: v for k, v in _L2_ffn_all.items() if k in ('Ws', 'bs', 'W1', 'b1', 'W2', 'b2')}
    del _L2_ffn_all

    def _L3_attn_setup():
        import jax, jax.numpy as jnp
        import numpy as np
        B, S, H = (2, 512, 256)
        NUM_HEADS = 16
        HEAD_DIM = H // NUM_HEADS
        key = jax.random.key(seed)
        ks = jax.random.split(key, 5)
        sc = 1.0 / np.sqrt(H)
        return {'hidden_states': jax.random.normal(ks[0], (B, S, H), jnp.float32), 'Wq': jax.random.normal(ks[1], (H, H), jnp.float32) * sc, 'bq': jnp.zeros((H,), jnp.float32), 'Wk': jax.random.normal(ks[2], (H, H), jnp.float32) * sc, 'bk': jnp.zeros((H,), jnp.float32), 'Wv': jax.random.normal(ks[3], (H, H), jnp.float32) * sc, 'bv': jnp.zeros((H,), jnp.float32), 'Wg': jax.random.normal(ks[4], (H, 1), jnp.float32) * sc, 'bg': jnp.zeros((1,), jnp.float32)}
    _L3_attn_all = _L3_attn_setup()
    _L3_attn_in = {k: v for k, v in _L3_attn_all.items() if k in ('Wq', 'bq', 'Wk', 'bk', 'Wv', 'bv', 'Wg', 'bg')}
    del _L3_attn_all

    def _L3_xattn_setup():
        import jax, jax.numpy as jnp
        import numpy as np
        B, NQ, NK = (2, 512, 512)
        DIM_Q = DIM_KV = DIM_E = DIM_O = 256
        H = 16
        HD = DIM_E // H
        SCALE = HD ** (-0.5)
        key = jax.random.key(seed)
        ks = jax.random.split(key, 8)
        inp = {'query': jax.random.normal(ks[0], (B, NQ, DIM_Q), dtype=jnp.float32), 'key': jax.random.normal(ks[1], (B, NK, DIM_KV), dtype=jnp.float32), 'value': jax.random.normal(ks[2], (B, NK, DIM_KV), dtype=jnp.float32), 'Wq': jax.random.normal(ks[3], (DIM_Q, DIM_E), dtype=jnp.float32) * DIM_Q ** (-0.5), 'Wk': jax.random.normal(ks[4], (DIM_KV, DIM_E), dtype=jnp.float32) * DIM_KV ** (-0.5), 'Wv': jax.random.normal(ks[5], (DIM_KV, DIM_E), dtype=jnp.float32) * DIM_KV ** (-0.5), 'Wo': jax.random.normal(ks[6], (DIM_E, DIM_O), dtype=jnp.float32) * DIM_E ** (-0.5), 'bo': jax.random.normal(ks[7], (DIM_O,), dtype=jnp.float32) * 0.01}
        return inp
    _L3_xattn_all = _L3_xattn_setup()
    _L3_xattn_in = {k: v for k, v in _L3_xattn_all.items() if k in ('Wq', 'Wk', 'Wv', 'Wo', 'bo')}
    del _L3_xattn_all

    def _L3_ffn_setup():
        import jax, jax.numpy as jnp
        import numpy as np
        B, S, H, E, K, I = (4, 512, 256, 8, 2, 1024)
        GATE_EPS = 1e-06
        LN_EPS = 1e-05
        key = jax.random.key(seed)
        k0, k1, k2, k3 = jax.random.split(key, 4)
        x = jax.random.normal(k0, (B, S, H), jnp.float32)
        gate_w = jax.random.normal(k1, (E, H), jnp.float32) * np.float32(np.sqrt(2.0 / (H + E)))
        expert_bias = jnp.zeros((E,), jnp.float32)
        w_up = jax.random.normal(k2, (E, I, H), jnp.float32) * np.float32(np.sqrt(2.0 / (H + I)))
        w_down = jax.random.normal(k3, (E, H, I), jnp.float32) * np.float32(np.sqrt(2.0 / (H + I)))
        return {'x': x, 'gate_w': gate_w, 'expert_bias': expert_bias, 'w_up': w_up, 'w_down': w_down}
    _L3_ffn_all = _L3_ffn_setup()
    _L3_ffn_in = {k: v for k, v in _L3_ffn_all.items() if k in ('gate_w', 'expert_bias', 'w_up', 'w_down')}
    del _L3_ffn_all
    return {'x': x, 'ctx_1024': ctx_1024, 'mask_BxSxS2_if1': mask_BxSxS2_if1, 'L0_attn_W_u': _L0_attn_in['W_u'], 'L0_attn_b_u': _L0_attn_in['b_u'], 'L0_attn_W_g': _L0_attn_in['W_g'], 'L0_attn_b_g': _L0_attn_in['b_g'], 'L0_attn_A': _L0_attn_in['A'], 'L0_attn_Bm': _L0_attn_in['Bm'], 'L0_attn_Cm': _L0_attn_in['Cm'], 'L0_attn_D': _L0_attn_in['D'], 'L0_xattn_tab_g': _L0_xattn_in['tab_g'], 'L0_xattn_tab_b': _L0_xattn_in['tab_b'], 'L0_xattn_vid_g': _L0_xattn_in['vid_g'], 'L0_xattn_vid_b': _L0_xattn_in['vid_b'], 'L0_xattn_Wq': _L0_xattn_in['Wq'], 'L0_xattn_Wk': _L0_xattn_in['Wk'], 'L0_xattn_Wv': _L0_xattn_in['Wv'], 'L0_xattn_q_g': _L0_xattn_in['q_g'], 'L0_xattn_q_b': _L0_xattn_in['q_b'], 'L0_xattn_k_g': _L0_xattn_in['k_g'], 'L0_xattn_k_b': _L0_xattn_in['k_b'], 'L0_xattn_Wo': _L0_xattn_in['Wo'], 'L0_xattn_bo': _L0_xattn_in['bo'], 'L0_ffn_w_gate': _L0_ffn_in['w_gate'], 'L0_ffn_w_up': _L0_ffn_in['w_up'], 'L0_ffn_w_down': _L0_ffn_in['w_down'], 'L1_attn_w_in': _L1_attn_in['w_in'], 'L1_attn_b_in': _L1_attn_in['b_in'], 'L1_attn_w_conv': _L1_attn_in['w_conv'], 'L1_attn_b_conv': _L1_attn_in['b_conv'], 'L1_attn_w_x': _L1_attn_in['w_x'], 'L1_attn_b_x': _L1_attn_in['b_x'], 'L1_attn_w_out': _L1_attn_in['w_out'], 'L1_attn_b_out': _L1_attn_in['b_out'], 'L1_xattn_Wq': _L1_xattn_in['Wq'], 'L1_xattn_bq': _L1_xattn_in['bq'], 'L1_xattn_Wk': _L1_xattn_in['Wk'], 'L1_xattn_bk': _L1_xattn_in['bk'], 'L1_xattn_Wv': _L1_xattn_in['Wv'], 'L1_xattn_bv': _L1_xattn_in['bv'], 'L1_xattn_Wo': _L1_xattn_in['Wo'], 'L1_xattn_bo': _L1_xattn_in['bo'], 'L1_ffn_w_router': _L1_ffn_in['w_router'], 'L1_ffn_w_up': _L1_ffn_in['w_up'], 'L1_ffn_w_gate': _L1_ffn_in['w_gate'], 'L1_ffn_w_down': _L1_ffn_in['w_down'], 'L1_ffn_ws_up': _L1_ffn_in['ws_up'], 'L1_ffn_ws_gate': _L1_ffn_in['ws_gate'], 'L1_ffn_ws_down': _L1_ffn_in['ws_down'], 'L2_attn_Wq': _L2_attn_in['Wq'], 'L2_attn_Wk': _L2_attn_in['Wk'], 'L2_attn_Wv': _L2_attn_in['Wv'], 'L2_attn_Wo': _L2_attn_in['Wo'], 'L2_xattn_w_q': _L2_xattn_in['w_q'], 'L2_xattn_w_k': _L2_xattn_in['w_k'], 'L2_xattn_w_v': _L2_xattn_in['w_v'], 'L2_xattn_w_o': _L2_xattn_in['w_o'], 'L2_xattn_b_o': _L2_xattn_in['b_o'], 'L2_ffn_Ws': _L2_ffn_in['Ws'], 'L2_ffn_bs': _L2_ffn_in['bs'], 'L2_ffn_W1': _L2_ffn_in['W1'], 'L2_ffn_b1': _L2_ffn_in['b1'], 'L2_ffn_W2': _L2_ffn_in['W2'], 'L2_ffn_b2': _L2_ffn_in['b2'], 'L3_attn_Wq': _L3_attn_in['Wq'], 'L3_attn_bq': _L3_attn_in['bq'], 'L3_attn_Wk': _L3_attn_in['Wk'], 'L3_attn_bk': _L3_attn_in['bk'], 'L3_attn_Wv': _L3_attn_in['Wv'], 'L3_attn_bv': _L3_attn_in['bv'], 'L3_attn_Wg': _L3_attn_in['Wg'], 'L3_attn_bg': _L3_attn_in['bg'], 'L3_xattn_Wq': _L3_xattn_in['Wq'], 'L3_xattn_Wk': _L3_xattn_in['Wk'], 'L3_xattn_Wv': _L3_xattn_in['Wv'], 'L3_xattn_Wo': _L3_xattn_in['Wo'], 'L3_xattn_bo': _L3_xattn_in['bo'], 'L3_ffn_gate_w': _L3_ffn_in['gate_w'], 'L3_ffn_expert_bias': _L3_ffn_in['expert_bias'], 'L3_ffn_w_up': _L3_ffn_in['w_up'], 'L3_ffn_w_down': _L3_ffn_in['w_down']}

def reference(x, ctx_1024, mask_BxSxS2_if1, L0_attn_W_u, L0_attn_b_u, L0_attn_W_g, L0_attn_b_g, L0_attn_A, L0_attn_Bm, L0_attn_Cm, L0_attn_D, L0_xattn_tab_g, L0_xattn_tab_b, L0_xattn_vid_g, L0_xattn_vid_b, L0_xattn_Wq, L0_xattn_Wk, L0_xattn_Wv, L0_xattn_q_g, L0_xattn_q_b, L0_xattn_k_g, L0_xattn_k_b, L0_xattn_Wo, L0_xattn_bo, L0_ffn_w_gate, L0_ffn_w_up, L0_ffn_w_down, L1_attn_w_in, L1_attn_b_in, L1_attn_w_conv, L1_attn_b_conv, L1_attn_w_x, L1_attn_b_x, L1_attn_w_out, L1_attn_b_out, L1_xattn_Wq, L1_xattn_bq, L1_xattn_Wk, L1_xattn_bk, L1_xattn_Wv, L1_xattn_bv, L1_xattn_Wo, L1_xattn_bo, L1_ffn_w_router, L1_ffn_w_up, L1_ffn_w_gate, L1_ffn_w_down, L1_ffn_ws_up, L1_ffn_ws_gate, L1_ffn_ws_down, L2_attn_Wq, L2_attn_Wk, L2_attn_Wv, L2_attn_Wo, L2_xattn_w_q, L2_xattn_w_k, L2_xattn_w_v, L2_xattn_w_o, L2_xattn_b_o, L2_ffn_Ws, L2_ffn_bs, L2_ffn_W1, L2_ffn_b1, L2_ffn_W2, L2_ffn_b2, L3_attn_Wq, L3_attn_bq, L3_attn_Wk, L3_attn_bk, L3_attn_Wv, L3_attn_bv, L3_attn_Wg, L3_attn_bg, L3_xattn_Wq, L3_xattn_Wk, L3_xattn_Wv, L3_xattn_Wo, L3_xattn_bo, L3_ffn_gate_w, L3_ffn_expert_bias, L3_ffn_w_up, L3_ffn_w_down):
    import jax
    import jax.numpy as jnp

    def _L0_attn_ref(x, W_u, b_u, W_g, b_g, A, Bm, Cm, D):
        import jax, jax.numpy as jnp
        import numpy as np
        B_SZ, T, D_IN, H = (8, 256, 256, 256)
        u = jax.nn.gelu(jnp.einsum('btd,hd->bth', x, W_u) + b_u, approximate=False) * jax.nn.sigmoid(jnp.einsum('btd,hd->bth', x, W_g) + b_g)
        uB = jnp.einsum('btd,hd->tbh', u, Bm)

        def step(s, uB_t):
            s = s @ A.T + uB_t
            y = s @ Cm.T + D
            return (s, y)
        s0 = jnp.zeros((x.shape[0], A.shape[0]), dtype=x.dtype)
        _, ys = jax.lax.scan(step, s0, uB)
        return jnp.transpose(ys, (1, 0, 2))

    def _L0_xattn_ref(x, tab_x, tab_g, tab_b, vid_g, vid_b, Wq, Wk, Wv, q_g, q_b, k_g, k_b, Wo, bo):
        import jax, jax.numpy as jnp
        import numpy as np
        EPS = 1e-05

        def layernorm(x, g, b):
            mu = jnp.mean(x, axis=-1, keepdims=True)
            var = jnp.var(x, axis=-1, keepdims=True)
            return (x - mu) * jax.lax.rsqrt(var + EPS) * g + b
        DIM = 256
        CTX = 256
        HEADS = 12
        DHEAD = 64
        INNER = HEADS * DHEAD
        B = 4
        F = 512
        J = 256
        scale = DHEAD ** (-0.5)
        kv_in = layernorm(tab_x, tab_g, tab_b)
        q = layernorm(layernorm(x, vid_g, vid_b) @ Wq, q_g, q_b)
        k = layernorm(kv_in @ Wk, k_g, k_b)
        v = kv_in @ Wv
        split = lambda t: t.reshape(t.shape[0], t.shape[1], HEADS, DHEAD).transpose(0, 2, 1, 3)
        q, k, v = (split(q) * scale, split(k), split(v))
        sim = jnp.einsum('bhid,bhjd->bhij', q, k)
        attn = jax.nn.softmax(sim, axis=-1)
        out = jnp.einsum('bhij,bhjd->bhid', attn, v)
        out = out.transpose(0, 2, 1, 3).reshape(x.shape[0], x.shape[1], INNER)
        return out @ Wo + bo

    def _L0_ffn_ref(x, w_gate, w_up, w_down):
        import jax, jax.numpy as jnp
        import numpy as np
        HIDDEN = 256
        INNER = 1024

        def _weight_quant(w):
            scale = 1.0 / jnp.clip(jnp.mean(jnp.abs(w)), 1e-05)
            wq = jnp.clip(jnp.round(w * scale), -1.0, 1.0) / scale
            return w + jax.lax.stop_gradient(wq - w)

        def _act_quant(x):
            scale = 127.0 / jnp.clip(jnp.max(jnp.abs(x), axis=-1, keepdims=True), 1e-05)
            xq = jnp.clip(jnp.round(x * scale), -128.0, 127.0) / scale
            return x + jax.lax.stop_gradient(xq - x)

        def _bitlinear(x, w):
            return jnp.einsum('bsi,oi->bso', _act_quant(x), _weight_quant(w))
        gate = jax.nn.silu(_bitlinear(x, w_gate))
        up = _bitlinear(x, w_up)
        return _bitlinear(gate * up, w_down)

    def _L1_attn_ref(x, w_in, b_in, w_conv, b_conv, w_x, b_x, w_out, b_out):
        import jax, jax.numpy as jnp
        import numpy as np
        D_MODEL, D_STATE, D_INNER = (256, 16, 512)
        EPS = 1e-05

        def bit_linear(x, w, b):
            scale = jnp.maximum(jnp.mean(jnp.abs(w)), EPS)
            ws = w / scale
            wq = ws + jax.lax.stop_gradient(jnp.clip(jnp.round(ws), -1.0, 1.0) - ws)
            return jnp.einsum('bsd,od->bso', x, wq) * scale + b

        def causal_dwconv(x, w, b):
            xc = jnp.transpose(x, (0, 2, 1))
            y = jax.lax.conv_general_dilated(xc, w, window_strides=(1,), padding=[(3, 0)], feature_group_count=w.shape[0], dimension_numbers=('NCH', 'OIH', 'NCH'))
            y = y + b[None, :, None]
            return jnp.transpose(y, (0, 2, 1))
        x_and_res = bit_linear(x, w_in, b_in)
        x_inner = x_and_res[..., :D_INNER]
        x_conv = jax.nn.silu(causal_dwconv(x_inner, w_conv, b_conv))
        ssm_params = bit_linear(x_conv, w_x, b_x)
        delta = ssm_params[..., :D_INNER]
        gate = jax.nn.sigmoid(delta)
        y = x_conv * gate
        return bit_linear(y, w_out, b_out)

    def _L1_xattn_ref(query, key, value, Wq, bq, Wk, bk, Wv, bv, Wo, bo):
        import jax, jax.numpy as jnp
        import numpy as np
        DIM = 256
        N_HEADS = 16
        HEAD_DIM = DIM // N_HEADS
        GAMMA = 10.0

        def larope_cos_sin(seq_len, gamma, head_dim):
            inv_freq = 1.0 / 10000.0 ** (jnp.arange(0, head_dim, 2, dtype=jnp.float32) / head_dim)
            t = jnp.arange(seq_len, dtype=jnp.float32)
            freqs = jnp.outer(gamma * (t / seq_len), inv_freq)
            emb = jnp.concatenate([freqs, freqs], axis=-1)
            return (jnp.cos(emb), jnp.sin(emb))

        def apply_rope(x, cos, sin):
            d = x.shape[-1] // 2
            x1, x2 = (x[..., :d], x[..., d:])
            c = cos[None, None, :, :d]
            s = sin[None, None, :, :d]
            return jnp.concatenate([x1 * c - x2 * s, x1 * s + x2 * c], axis=-1)
        B, Lq, _ = query.shape
        Lk = key.shape[1]
        scale = HEAD_DIM ** (-0.5)

        def proj(x, W, b, L):
            y = x @ W.T + b
            return y.reshape(B, L, N_HEADS, HEAD_DIM).transpose(0, 2, 1, 3)
        q = proj(query, Wq, bq, Lq)
        k = proj(key, Wk, bk, Lk)
        v = proj(value, Wv, bv, Lk)
        q_cos, q_sin = larope_cos_sin(Lq, GAMMA, HEAD_DIM)
        k_cos, k_sin = larope_cos_sin(Lk, GAMMA, HEAD_DIM)
        q = apply_rope(q, q_cos, q_sin)
        k = apply_rope(k, k_cos, k_sin)
        scores = jnp.einsum('bhqd,bhkd->bhqk', q, k) * scale
        attn = jax.nn.softmax(scores, axis=-1)
        out = jnp.einsum('bhqk,bhkd->bhqd', attn, v)
        out = out.transpose(0, 2, 1, 3).reshape(B, Lq, DIM)
        return out @ Wo.T + bo

    def _L1_ffn_ref(x, w_router, w_up, w_gate, w_down, ws_up, ws_gate, ws_down):
        import jax, jax.numpy as jnp
        import numpy as np
        DIM = 256
        HID = 1024
        E = 8
        TOPK = 2
        ALPHA = 2.0
        B, T = (1, 512)
        DOWN_SCALE = 0.01
        logits = x @ w_router
        probs = jax.nn.softmax(logits.astype(jnp.float32), axis=-1).astype(logits.dtype)
        topk_vals, topk_idx = jax.lax.top_k(probs, TOPK)
        up = jnp.einsum('btd,edh->ebth', x, w_up)
        gate = jax.nn.silu(jnp.einsum('btd,edh->ebth', x, w_gate))
        exp_out = jnp.einsum('ebth,ehd->ebtd', up * gate, w_down)
        out = jnp.zeros_like(x)
        eids = jnp.arange(E - 1)
        for i in range(TOPK - 1):
            idx_i = topk_idx[..., i]
            sel = (idx_i[None, :, :] == eids[:, None, None]).astype(x.dtype)
            gathered = jnp.einsum('ebt,ebtd->btd', sel, exp_out)
            out = out + ALPHA * topk_vals[..., i:i + 1] * gathered
        shared = x @ ws_up * jax.nn.silu(x @ ws_gate) @ ws_down
        return out + shared

    def _L2_attn_ref(x, Wq, Wk, Wv, Wo):
        import jax, jax.numpy as jnp
        import numpy as np
        B, T, E = (4, 512, 256)
        H, D = (8, 128)

        def sinusoidal_pe(length, dim, dtype=jnp.float32):
            pos = jnp.arange(length, dtype=jnp.float32)[:, None]
            inv_freq = jnp.exp(-jnp.log(jnp.float32(10000.0)) * (jnp.arange(0, dim, 2, dtype=jnp.float32) / dim))
            ang = pos * inv_freq[None, :]
            pe = jnp.zeros((length, dim), dtype=jnp.float32)
            pe = pe.at[:, 0::2].set(jnp.sin(ang)).at[:, 1::2].set(jnp.cos(ang))
            return pe.astype(dtype)
        Bv, Tv, Ev = x.shape
        scale = 1.0 / jnp.sqrt(jnp.float32(D)).astype(x.dtype)
        q = (x @ Wq.T).reshape(Bv, Tv, H, D)
        k = (x @ Wk.T).reshape(Bv, Tv, 1, D)
        v = (x @ Wv.T).reshape(Bv, Tv, 1, D)
        k = k + sinusoidal_pe(1, D, k.dtype)
        q = jnp.transpose(q, (0, 2, 1, 3))
        k1 = k[:, :, 0, :]
        v1 = v[:, :, 0, :]
        q = q + sinusoidal_pe(Tv, D, q.dtype)[None, None]
        scores = jnp.einsum('bhtd,bsd->bhts', q, k1) * scale
        causal = jnp.tril(jnp.ones((Tv, Tv), dtype=bool))
        scores = jnp.where(causal[None, None], scores, jnp.finfo(scores.dtype).min)
        probs = jax.nn.softmax(scores, axis=-1)
        attn = jnp.einsum('bhts,bsd->bhtd', probs, v1)
        out = jnp.transpose(attn, (0, 2, 1, 3)).reshape(Bv, Tv, H * D)
        return out @ Wo.T

    def _L2_xattn_ref(q, k, v, mask, w_q, w_k, w_v, w_o, b_o):
        import jax, jax.numpy as jnp
        import numpy as np
        D_MODEL = 256
        HEADS = 16
        D_K = D_MODEL // HEADS
        B, S, _ = q.shape

        def split_heads(x, w):
            y = jnp.einsum('bse,de->bsd', x, w)
            return y.reshape(B, S, HEADS, D_K).transpose(0, 2, 1, 3)
        qh, kh, vh = (split_heads(q, w_q), split_heads(k, w_k), split_heads(v, w_v))
        score = jnp.einsum('bhqd,bhkd->bhqk', qh, kh) / jnp.sqrt(jnp.float32(D_K))
        score = jnp.where(mask[:, None, :, :] == 0, -jnp.inf, score)
        attn = jax.nn.softmax(score, axis=-1)
        out = jnp.einsum('bhqk,bhkd->bhqd', attn, vh)
        out = out.transpose(0, 2, 1, 3).reshape(B, S, HEADS * D_K)
        return jnp.einsum('bsd,ed->bse', out, w_o) + b_o

    def _L2_ffn_ref(x, Ws, bs, W1, b1, W2, b2):
        import jax, jax.numpy as jnp
        import numpy as np
        CAPACITY_FACTOR = 1.0
        B, S, D = x.shape
        E = Ws.shape[1]
        N = B * S
        k = int(CAPACITY_FACTOR * N / E)
        xf = x.reshape(N, D)
        route_prob = jax.nn.softmax(xf @ Ws + bs, axis=-1).T
        route_vals, routes = jax.lax.top_k(route_prob, k)
        xin = xf[routes]
        h = jax.nn.gelu(jnp.einsum('ekd,edf->ekf', xin, W1) + b1[:, None, :])
        out = jnp.einsum('ekf,efd->ekd', h, W2) + b2[:, None, :]
        out = out * route_vals[..., None]
        final = jnp.zeros((N, D), dtype=x.dtype).at[routes.reshape(-1)].add(out.reshape(-1, D))
        return final.reshape(B, S, D)

    def _L3_attn_ref(hidden_states, Wq, bq, Wk, bk, Wv, bv, Wg, bg):
        import jax, jax.numpy as jnp
        import numpy as np
        B, S, H = (2, 512, 256)
        NUM_HEADS = 16
        HEAD_DIM = H // NUM_HEADS
        b, s, h = hidden_states.shape
        g = jax.nn.sigmoid(hidden_states @ Wg + bg)
        Z_I = g
        Z_J = jnp.swapaxes(g, 1, 2)
        res = (1.0 - Z_I) * jnp.maximum(1.0 - Z_I - Z_J, 0.0) + Z_I * jnp.minimum(1.0 - Z_I + Z_J, 1.0)
        idx = jnp.arange(s)
        abs_ij = jnp.abs(idx[:, None] - idx[None, :]).astype(hidden_states.dtype)
        base = jnp.asarray(s - 2, hidden_states.dtype)
        scope = jnp.power(base, 1.0 - g) + 2.0 - abs_ij
        scope = jnp.clip(scope, 1e-32, 1.0)
        penalties = res * scope
        log_pen = jnp.log(jnp.maximum(penalties, 1e-32))

        def split_heads(x):
            return x.reshape(b, s, NUM_HEADS, HEAD_DIM).transpose(0, 2, 1, 3)
        q = split_heads(hidden_states @ Wq + bq)
        k = split_heads(hidden_states @ Wk + bk)
        v = split_heads(hidden_states @ Wv + bv)
        scores = jnp.einsum('bhqd,bhkd->bhqk', q, k) / np.sqrt(HEAD_DIM)
        scores = scores + log_pen[:, None, :, :]
        probs = jax.nn.softmax(scores, axis=-1)
        ctx = jnp.einsum('bhqk,bhkd->bhqd', probs, v)
        ctx = ctx.transpose(0, 2, 1, 3).reshape(b, s, h)
        return ctx

    def _L3_xattn_ref(query, key, value, Wq, Wk, Wv, Wo, bo):
        import jax, jax.numpy as jnp
        import numpy as np
        B, NQ, NK = (2, 512, 512)
        DIM_Q = DIM_KV = DIM_E = DIM_O = 256
        H = 16
        HD = DIM_E // H
        SCALE = HD ** (-0.5)
        b, nq, _ = query.shape
        nk = key.shape[1]
        q = (query @ Wq).reshape(b, nq, H, HD).transpose(0, 2, 1, 3)
        k = (key @ Wk).reshape(b, nk, H, HD).transpose(0, 2, 1, 3)
        v = (value @ Wv).reshape(b, nk, H, HD).transpose(0, 2, 1, 3)
        attn = jnp.einsum('bhqd,bhkd->bhqk', q, k) * SCALE
        attn = jax.nn.softmax(attn, axis=-1)
        x = jnp.einsum('bhqk,bhkd->bhqd', attn, v)
        x = x.transpose(0, 2, 1, 3).reshape(b, nq, H * HD)
        return x @ Wo + bo

    def _L3_ffn_ref(x, gate_w, expert_bias, w_up, w_down):
        import jax, jax.numpy as jnp
        import numpy as np
        B, S, H, E, K, I = (4, 512, 256, 8, 2, 1024)
        GATE_EPS = 1e-06
        LN_EPS = 1e-05
        logits = jnp.einsum('bsh,eh->bse', x, gate_w) + expert_bias
        weights = jax.nn.softmax(logits, axis=-1)
        top_w, top_i = jax.lax.top_k(weights, K)
        top_w = top_w / (jnp.sum(top_w, axis=-1, keepdims=True) + GATE_EPS)
        sparse_w = jnp.sum(jax.nn.one_hot(top_i, E, dtype=weights.dtype) * top_w[..., None], axis=-2)
        out = jnp.zeros_like(x)
        for e in range(E):
            h = jax.nn.gelu(jnp.einsum('bsh,ih->bsi', x, w_up[e]), approximate=False)
            y = jnp.einsum('bsi,hi->bsh', h, w_down[e])
            out = out + sparse_w[..., e:e + 1] * y
        mu = jnp.mean(out, axis=-1, keepdims=True)
        var = jnp.mean(jnp.square(out - mu), axis=-1, keepdims=True)
        out = (out - mu) * jax.lax.rsqrt(var + LN_EPS)
        return out + x
    x = _layernorm(x + _L0_attn_ref(x, L0_attn_W_u, L0_attn_b_u, L0_attn_W_g, L0_attn_b_g, L0_attn_A, L0_attn_Bm, L0_attn_Cm, L0_attn_D), axis=-1)
    x = _layernorm(x + _L0_xattn_ref(x, ctx_1024, L0_xattn_tab_g, L0_xattn_tab_b, L0_xattn_vid_g, L0_xattn_vid_b, L0_xattn_Wq, L0_xattn_Wk, L0_xattn_Wv, L0_xattn_q_g, L0_xattn_q_b, L0_xattn_k_g, L0_xattn_k_b, L0_xattn_Wo, L0_xattn_bo), axis=-1)
    x = _layernorm(x + _L0_ffn_ref(x, L0_ffn_w_gate, L0_ffn_w_up, L0_ffn_w_down), axis=-1)
    x = _layernorm(x + _L1_attn_ref(x, L1_attn_w_in, L1_attn_b_in, L1_attn_w_conv, L1_attn_b_conv, L1_attn_w_x, L1_attn_b_x, L1_attn_w_out, L1_attn_b_out), axis=-1)
    x = _layernorm(x + _L1_xattn_ref(x, ctx_1024, ctx_1024, L1_xattn_Wq, L1_xattn_bq, L1_xattn_Wk, L1_xattn_bk, L1_xattn_Wv, L1_xattn_bv, L1_xattn_Wo, L1_xattn_bo), axis=-1)
    x = _layernorm(x + _L1_ffn_ref(x, L1_ffn_w_router, L1_ffn_w_up, L1_ffn_w_gate, L1_ffn_w_down, L1_ffn_ws_up, L1_ffn_ws_gate, L1_ffn_ws_down), axis=-1)
    x = _layernorm(x + _L2_attn_ref(x, L2_attn_Wq, L2_attn_Wk, L2_attn_Wv, L2_attn_Wo), axis=-1)
    x = _layernorm(x + _L2_xattn_ref(x, ctx_1024, ctx_1024, mask_BxSxS2_if1, L2_xattn_w_q, L2_xattn_w_k, L2_xattn_w_v, L2_xattn_w_o, L2_xattn_b_o), axis=-1)
    x = _layernorm(x + _L2_ffn_ref(x, L2_ffn_Ws, L2_ffn_bs, L2_ffn_W1, L2_ffn_b1, L2_ffn_W2, L2_ffn_b2), axis=-1)
    x = _layernorm(x + _L3_attn_ref(x, L3_attn_Wq, L3_attn_bq, L3_attn_Wk, L3_attn_bk, L3_attn_Wv, L3_attn_bv, L3_attn_Wg, L3_attn_bg), axis=-1)
    x = _layernorm(x + _L3_xattn_ref(x, ctx_1024, ctx_1024, L3_xattn_Wq, L3_xattn_Wk, L3_xattn_Wv, L3_xattn_Wo, L3_xattn_bo), axis=-1)
    x = _layernorm(x + _L3_ffn_ref(x, L3_ffn_gate_w, L3_ffn_expert_bias, L3_ffn_w_up, L3_ffn_w_down), axis=-1)
    return x

_drawn_inputs = setup_inputs


def setup_inputs(seed=0):
    import zlib

    import numpy as np

    out = dict(_drawn_inputs(seed))
    spreads = {'L0_xattn_tab_g': (1.0, 0.2),
     'L0_xattn_tab_b': (0.0, 0.1),
     'L0_xattn_vid_g': (1.0, 0.2),
     'L0_xattn_vid_b': (0.0, 0.1),
     'L0_xattn_q_g': (1.0, 0.2),
     'L0_xattn_q_b': (0.0, 0.1),
     'L0_xattn_k_g': (1.0, 0.2),
     'L0_xattn_k_b': (0.0, 2.0),
     'L0_xattn_bo': (0.0, 0.1),
     'L1_xattn_bq': (0.0, 0.1),
     'L1_xattn_bk': (0.0, 0.343),
     'L1_xattn_bv': (0.0, 0.1),
     'L1_xattn_bo': (0.0, 0.1),
     'L2_xattn_b_o': (0.0, 0.1),
     'L2_ffn_bs': (0.0, 0.1),
     'L2_ffn_b1': (0.0, 0.1),
     'L2_ffn_b2': (0.0, 0.1),
     'L3_attn_bq': (0.0, 0.314),
     'L3_attn_bk': (0.0, 2.0),
     'L3_attn_bv': (0.0, 0.1),
     'L3_ffn_expert_bias': (0.0, 0.1)}
    factors = {'L1_attn_b_in': 8.0,
     'L1_attn_w_conv': 2.836,
     'L1_attn_b_conv': 4.854,
     'L1_attn_w_x': 22.973,
     'L1_attn_b_x': 26.602,
     'L2_attn_Wq': 4.0,
     'L2_attn_Wk': 2.717}
    for name, (base, spread) in spreads.items():
        noise = np.random.default_rng([zlib.crc32(name.encode()), seed]).standard_normal(out[name].shape)
        drawn = base * np.exp(spread * noise) if base else spread * noise
        out[name] = jnp.asarray(drawn.astype(out[name].dtype))
    for name, factor in factors.items():
        out[name] = (out[name] * factor).astype(out[name].dtype)
    return out
```

```python
import math
from contextlib import ExitStack

import numpy as np

import concourse.bass as bass
from concourse import mybir

ALU = mybir.AluOpType
ACT = mybir.ActivationFunctionType
AX = mybir.AxisListType
F32 = mybir.dt.float32
BF16 = mybir.dt.bfloat16
I32 = mybir.dt.int32
U32 = mybir.dt.uint32

P = 128
NB = 16
D = 256
KD = D // P
G = 4
NG = NB // G
GT = G * P
LN_EPS = 1e-5
MASKED = -3.0e38


class Core:

    def __init__(self, nc, ctx):
        self.nc = nc
        self.spent = []
        self.X = ctx.enter_context(nc.sbuf_tensor("X", [P, NB, D], F32))
        self.XT = ctx.enter_context(nc.sbuf_tensor("XT", [P, KD, NB * P], F32))
        self.CT = ctx.enter_context(nc.sbuf_tensor("CT", [P, KD, NB * P], F32))
        self.ident = ctx.enter_context(nc.sbuf_tensor("ident", [P, P], F32))
        self.ones = ctx.enter_context(nc.sbuf_tensor("ones", [P, P], F32))
        self.held = ctx.enter_context(nc.semaphore("held"))
        self.mhalf = ctx.enter_context(nc.sbuf_tensor("mhalf", [P, 1], F32))


def hold(eng, core):
    eng.sem_inc(core.held, 1)


class Stage:

    def __init__(self, core, name):
        self.core, self.nc, self.name = core, core.nc, name
        self.ctx = ExitStack()
        self.primed, self.sems = [], []

    def __enter__(self):
        self.ctx.__enter__()
        return self

    def __exit__(self, *a):
        ended = self.ctx.__exit__(*a)
        core = self.core
        core.spent += self.sems
        if len(core.spent) > 90:
            self.nc.clear_and_free_semaphores(core.spent)
            self.nc.all_engine_barrier()
            core.spent = []
        return ended

    def sb(self, name, shape, dt=F32):
        return self.ctx.enter_context(self.nc.sbuf_tensor(f"{self.name}_{name}", shape, dt))

    def ps(self, name, shape, dt=F32):
        return self.ctx.enter_context(self.nc.psum_tensor(f"{self.name}_{name}", shape, dt))

    def sem(self, name, primed=0):
        s = self.nc.alloc_semaphore(f"{self.name}_{name}")
        self.sems.append(s)
        if primed:
            self.primed.append((s, primed))
        return s

    def prime(self, eng):
        for s, n in self.primed:
            eng.sem_inc(s, n)

    def block(self):
        return self.ctx.enter_context(self.nc.Block())


class Steps:

    def __init__(self, eng, sem, per):
        self.eng, self.sem, self.per = eng, sem, per

    def turn(self, b):
        self.b, self.k = b, 0

    def then(self, ins):
        ins.then_inc(self.sem, 1)
        self.k += 1
        assert self.k <= self.per, "more steps than counted"
        self.eng.wait_ge(self.sem, self.b * self.per + self.k)

    def end(self):
        assert self.k == self.per, f"{self.k} steps, {self.per} counted"


class Tail:

    def __init__(self, s, core, T):
        self.s, self.core, self.T = s, core, T
        self.xres = s.sb("xres", [P, D])
        self.r = s.sb("r", [P, D])
        self.stats = s.sb("stats", [P, 6])
        self.mv = s.sb("mv", [P, 2])
        self.ve = s.sb("ve", [P, 1])
        self.rstd = s.sb("rstd", [P, 1])
        self.xn = s.sb("xn", [P, D])
        self.y_ready = s.sem("y_ready")
        self.y_used = s.sem("y_used", 1)
        self.xres_ready = s.sem("xres_ready")
        self.ve_ready = s.sem("ve_ready")
        self.rstd_ready = s.sem("rstd_ready")
        self.xn_ready = s.sem("xn_ready", 1)
        self.x_stored = s.sem("x_stored", 1)
        self.xT_ready = s.sem("xT_ready", 1)
        self.xT_stored = s.sem("xT_stored", 1)
        self.STEPS = 3

    def pool_residual(self, pool, b, bias=None):
        pool.wait_ge(self.y_used, b + 1)
        hold(pool, self.core)
        if bias is None:
            pool.tensor_copy(self.xres[:], self.core.X[:, b, :]).then_inc(self.xres_ready, 1)
        else:
            pool.tensor_tensor(self.xres[:], self.core.X[:, b, :], bias, ALU.add).then_inc(self.xres_ready, 1)

    def pool(self, pool, b):
        pool.wait_ge(self.ve_ready, b + 1)
        pool.tensor_tensor(self.rstd[:], self.ve[:], self.core.mhalf[:], ALU.pow).then_inc(self.rstd_ready, 1)
        pool.wait_ge(self.xn_ready, b + 2)
        hold(pool, self.core)
        pool.tensor_copy(self.core.X[:, b, :], self.xn[:]).then_inc(self.x_stored, 1)

    def vector(self, dve, steps, b, y, scale=None):
        dve.wait_ge(self.xn_ready, b + 1)
        dve.wait_ge(self.xres_ready, b + 1)
        dve.wait_ge(self.y_ready, b + 1)
        if scale is None:
            steps.then(dve.tensor_tensor(self.r[:], y, self.xres[:], ALU.add))
        else:
            steps.then(dve.scalar_tensor_tensor(out=self.r[:], in0=y, scalar=scale, in1=self.xres[:],
                                                op0=ALU.mult, op1=ALU.add))
        self.norm(dve, steps, b)

    def norm(self, dve, steps, b):
        steps.then(dve.bn_stats(self.stats[:], self.r[:]))
        dve.sem_inc(self.y_used, 1)
        steps.then(dve.bn_aggr(self.mv[:], self.stats[:]))
        dve.tensor_scalar(self.ve[:], self.mv[:, 1:2], LN_EPS, None, ALU.add).then_inc(self.ve_ready, 1)
        dve.wait_ge(self.xT_ready, b + 1)
        dve.wait_ge(self.x_stored, b + 1)
        dve.wait_ge(self.rstd_ready, b + 1)
        dve.tensor_scalar(self.xn[:], self.r[:], self.mv[:, 0:1], self.rstd[:], ALU.subtract,
                          ALU.mult).then_inc(self.xn_ready, 1)

    def tensor(self, pe, b):
        pe.wait_ge(self.xn_ready, b + 2)
        pe.wait_ge(self.xT_stored, b + 1)
        pe.transpose(self.T[:, 0, :], self.xn[:, 0:P], self.core.ident[:])
        pe.transpose(self.T[:, 1, :], self.xn[:, P:D], self.core.ident[:]).then_inc(self.xT_ready, 1)

    def scalar(self, act, b):
        act.wait_ge(self.xT_ready, b + 2)
        hold(act, self.core)
        act.copy(self.core.XT[:, :, bass.ts(b, P)], self.T[:]).then_inc(self.xT_stored, 1)


def rows(core, dst, src):
    return src.partition_broadcast(P)


def setup(core, a):
    with Stage(core, "setup") as s:
        loaded = s.sem("loaded")
        made = s.sem("made")
        block = s.block()

        @block.sync
        def _(sp):
            sp.dma_start(core.XT[:], a["xT"].rearrange("(k p) n -> p k n", p=P)).then_inc(loaded, 16)
            sp.dma_start(core.X[:], a["x"].rearrange("b t d -> t b d")).then_inc(loaded, 16)
            sp.dma_start(core.ident[:], a["c_ident"]).then_inc(loaded, 16)
            sp.dma_start(core.CT[:], a["ctxT"].rearrange("(k p) n -> p k n", p=P)).then_inc(loaded, 16)
            sp.wait_ge(loaded, 64)

        @block.gpsimd
        def _(pool):
            pool.memset(core.ones[:], 1.0).then_inc(made, 1)
            pool.memset(core.mhalf[:], -0.5).then_inc(made, 1)


def store(core, out):
    with Stage(core, "store") as s:
        stored = s.sem("stored")
        block = s.block()

        @block.sync
        def _(sp):
            sp.dma_start(out.rearrange("b t d -> t b d"), core.X[:]).then_inc(stored, 16)
            sp.wait_ge(stored, 16)


def l0_attn(core, a):
    J = 16
    NC = P // J
    Q = NB * NC
    with ExitStack() as keep:
        UB = keep.enter_context(core.nc.sbuf_tensor("scan_in", [P, KD, J, Q], F32))
        S = keep.enter_context(core.nc.sbuf_tensor("scan_state", [P, KD, J, Q], F32))
        l0_attn_inputs(core, a, UB, J, NC)
        l0_attn_scan(core, a, UB, S, J, NC, Q)
        l0_attn_out(core, a, S, NC)


def l0_attn_inputs(core, a, UB, J, NC):
    with Stage(core, "uin") as s:
        Wu, Wg, Bm = (s.sb(n, [P, KD, D]) for n in ("Wu", "Wg", "Bm"))
        bu, bg = (s.sb(n, [P, KD]) for n in ("bu", "bg"))
        gl, sg, u = (s.sb(n, [P, KD, GT]) for n in ("gl", "sg", "u"))
        pu, pg, pb = (s.ps(n, [P, KD, GT]) for n in ("pu", "pg", "pb"))
        loaded = s.sem("loaded")
        ug_ready = s.sem("ug_ready")
        gelu_ready = s.sem("gelu_ready", 1)
        sig_ready = s.sem("sig_ready", 1)
        u_ready = s.sem("u_ready", 1)
        ub_ready = s.sem("ub_ready", 1)
        ub_stored = s.sem("ub_stored", 1)
        block = s.block()

        @block.sync
        def _(sp):
            for dst, name in ((Wu, "L0_attn_W_uT"), (Wg, "L0_attn_W_gT"), (Bm, "L0_attn_BmT")):
                sp.dma_start(dst[:], a[name].rearrange("(k p) n -> p k n", p=P)).then_inc(loaded, 16)
            for dst, name in ((bu, "L0_attn_b_u_cols"), (bg, "L0_attn_b_g_cols")):
                sp.dma_start(dst[:], a[name]).then_inc(loaded, 16)
            sp.wait_ge(loaded, 80)

        @block.gpsimd
        def _(pool):
            s.prime(pool)

        @block.tensor
        def _(pe):
            pe.wait_ge(loaded, 80)
            with pe.Fori(0, NG) as g:
                pe.wait_ge(sig_ready, g + 1)
                for m in range(KD):
                    for w, out in ((Wu, pu), (Wg, pg)):
                        for k in range(KD):
                            ins = pe.matmul(out[:, m, :], w[:, k, bass.ts(m, P)], core.XT[:, k, bass.ts(g, GT)],
                                            start=(k == 0), stop=(k == KD - 1))
                ins.then_inc(ug_ready, 1)
                pe.wait_ge(ub_stored, g + 1)
                pe.wait_ge(u_ready, g + 2)
                for m in range(KD):
                    for k in range(KD):
                        ins = pe.matmul(pb[:, m, :], Bm[:, k, bass.ts(m, P)], u[:, k, :],
                                        start=(k == 0), stop=(k == KD - 1))
                ins.then_inc(ub_ready, 1)

        @block.scalar
        def _(act):
            act.wait_ge(loaded, 80)
            with act.Fori(0, NG) as g:
                act.wait_ge(u_ready, g + 1)
                act.wait_ge(ug_ready, g + 1)
                for m in range(KD):
                    ins = act.activation(gl[:, m, :], pu[:, m, :], ACT.Gelu, bias=bu[:, m:m + 1])
                ins.then_inc(gelu_ready, 1)
                for m in range(KD):
                    ins = act.activation(sg[:, m, :], pg[:, m, :], ACT.Sigmoid, bias=bg[:, m:m + 1])
                ins.then_inc(sig_ready, 1)

        @block.vector
        def _(dve):
            with dve.Fori(0, NG) as g:
                dve.wait_ge(ub_ready, g + 1)
                dve.wait_ge(sig_ready, g + 2)
                dve.tensor_tensor(u[:], gl[:], sg[:], ALU.mult).then_inc(u_ready, 1)
                dve.wait_ge(ub_ready, g + 2)
                for m in range(KD):
                    ins = dve.tensor_copy(UB[:, m, :, bass.ts(g, G * NC)],
                                          pb[:, m, :].rearrange("p (q j) -> p j q", j=J))
                ins.then_inc(ub_stored, 1)


def l0_attn_scan(core, a, UB, S, J, NC, Q):
    SQ = int(math.log2(J))
    with Stage(core, "scan") as s:
        pw = [(s.sb(f"At{n}", [P, KD, D]), s.sb(f"A{n}", [P, KD, D])) for n in range(2)]
        first = s.sb("first", [P, KD, NB, NC])
        ps = s.ps("ps", [P, KD, Q])
        pq = s.ps("pq", [P, 2, KD, D])
        loaded = s.sem("loaded")
        squares = s.sem("squares")
        power = s.sem("power")
        zeroed = s.sem("zeroed")
        carry_mm = s.sem("carry_mm")
        carried = s.sem("carried")
        started = s.sem("started")
        start_mm = s.sem("start_mm")
        step_mm = [s.sem("step_mm0"), s.sem("step_mm1")]
        stepped = [s.sem("stepped0"), s.sem("stepped1")]
        AT = pw[0][0]
        reload = s.sem("reload")
        block = s.block()

        @block.sync
        def _(sp):
            sp.dma_start(pw[0][0][:], a["L0_attn_AT"].rearrange("(k p) n -> p k n", p=P)).then_inc(loaded, 16)
            sp.dma_start(pw[0][1][:], a["L0_attn_A"].rearrange("(k p) n -> p k n", p=P)).then_inc(loaded, 16)
            sp.wait_ge(loaded, 32)

        A1 = s.sb("A1step", [P, KD, D])

        @block.scalar
        def _(act):
            act.wait_ge(loaded, 32)
            act.copy(A1[:], pw[0][0][:]).then_inc(reload, 1)
            for n in range(SQ):
                act.wait_ge(squares, n + 1)
                act.wait_ge(reload, 1)
                act.copy(pw[(n + 1) % 2][0][:], pq[:, 0, :, :])
                act.copy(pw[(n + 1) % 2][1][:], pq[:, 1, :, :]).then_inc(power, 1)

        @block.tensor
        def _(pe):
            pe.wait_ge(loaded, 32)
            for n in range(SQ):
                if n:
                    pe.wait_ge(power, n)
                At, A = pw[n % 2]
                for i, (l, r) in enumerate(((A, At), (At, A))):
                    for m in range(KD):
                        for k in range(KD):
                            ins = pe.matmul(pq[:, i, m, :], l[:, k, bass.ts(m, P)], r[:, k, :],
                                            start=(k == 0), stop=(k == KD - 1))
                ins.then_inc(squares, 1)
            AJ = pw[SQ % 2][0]
            pe.wait_ge(reload, 1)

            def steps(i):
                with pe.Fori(1, J) as j:
                    pe.wait_ge(stepped[i], j)
                    for m in range(KD):
                        for k in range(KD):
                            ins = pe.matmul(ps[:, m, :], A1[:, k, bass.ts(m, P)], S[:, k, j - 1, :],
                                            start=(k == 0), stop=(k == KD - 1))
                    ins.then_inc(step_mm[i], 1)

            steps(0)
            pe.wait_ge(power, SQ)
            for c in range(2, NC):
                pe.wait_ge(carried, c - 1)
                for m in range(KD):
                    for k in range(KD):
                        ins = pe.matmul(ps[:, m, 0:NB], AJ[:, k, bass.ts(m, P)], first[:, k, :, c - 1],
                                        start=(k == 0), stop=(k == KD - 1))
                ins.then_inc(carry_mm, 1)
            pe.wait_ge(carried, NC - 1)
            for m in range(KD):
                for k in range(KD):
                    ins = pe.matmul(ps[:, m, :], A1[:, k, bass.ts(m, P)],
                                    first[:, k, :, :].rearrange("p b c -> p (b c)"),
                                    start=(k == 0), stop=(k == KD - 1))
            ins.then_inc(start_mm, 1)
            steps(1)

        @block.vector
        def _(dve):
            dve.memset(first[:], 0.0).then_inc(zeroed, 1)
            dve.tensor_copy(S[:, :, 0, :], UB[:, :, 0, :]).then_inc(stepped[0], 1)

            def steps(i):
                with dve.Fori(1, J) as j:
                    dve.wait_ge(step_mm[i], j)
                    dve.tensor_tensor(S[:, :, j, :], ps[:], UB[:, :, j, :], ALU.add).then_inc(stepped[i], 1)

            steps(0)
            last = S[:, :, J - 1, :].rearrange("p k (b c) -> p k b c", c=NC)
            dve.wait_ge(stepped[0], J)
            dve.wait_ge(zeroed, 1)
            dve.tensor_copy(first[:, :, :, 1], last[:, :, :, 0]).then_inc(carried, 1)
            for c in range(2, NC):
                dve.wait_ge(carry_mm, c - 1)
                dve.tensor_tensor(first[:, :, :, c], ps[:, :, 0:NB], last[:, :, :, c - 1],
                                  ALU.add).then_inc(carried, 1)
            dve.wait_ge(start_mm, 1)
            dve.wait_ge(carried, NC - 1)
            dve.tensor_tensor(S[:, :, 0, :], ps[:], UB[:, :, 0, :], ALU.add).then_inc(stepped[1], 1)
            steps(1)


def l0_attn_out(core, a, S, NC):
    with Stage(core, "yout") as s:
        Cm = s.sb("Cm", [P, KD, D])
        Dt = s.sb("Dt", [P, D])
        sb_ = s.sb("state", [P, KD, P])
        y = s.ps("y", [P, D])
        T = s.ps("T", [P, KD, P])
        tail = Tail(s, core, T)
        loaded = s.sem("loaded")
        state_ready = s.sem("state_ready")
        self_steps = s.sem("vector_steps")
        block = s.block()

        @block.sync
        def _(sp):
            sp.dma_start(Cm[:], a["L0_attn_CmT"].rearrange("(k p) n -> p k n", p=P)).then_inc(loaded, 16)
            sp.dma_start(Dt[:], a["L0_attn_D"].partition_broadcast(P)).then_inc(loaded, 16)
            sp.wait_ge(loaded, 32)

        @block.gpsimd
        def _(pool):
            s.prime(pool)
            pool.wait_ge(loaded, 32)
            with pool.Fori(0, NB) as b:
                pool.wait_ge(tail.y_used, b + 1)
                hold(pool, core)
                for k in range(KD):
                    ins = pool.tensor_copy(sb_[:, k, :].rearrange("p (c j) -> p j c", c=NC),
                                           S[:, k, :, bass.ts(b, NC)])
                ins.then_inc(state_ready, 1)
                tail.pool_residual(pool, b, Dt[:])
                tail.pool(pool, b)

        @block.tensor
        def _(pe):
            pe.wait_ge(loaded, 32)
            with pe.Fori(0, NB) as b:
                pe.wait_ge(state_ready, b + 1)
                pe.wait_ge(tail.y_used, b + 1)
                for k in range(KD):
                    ins = pe.matmul(y[:], sb_[:, k, :], Cm[:, k, :], start=(k == 0), stop=(k == KD - 1))
                ins.then_inc(tail.y_ready, 1)
                tail.tensor(pe, b)

        @block.vector
        def _(dve):
            steps = Steps(dve, self_steps, tail.STEPS)
            with dve.Fori(0, NB) as b:
                steps.turn(b)
                tail.vector(dve, steps, b, y[:])
                steps.end()

        @block.scalar
        def _(act):
            with act.Fori(0, NB) as b:
                tail.scalar(act, b)


def l0_xattn(core, a):
    H, DHX = 12, 64
    INNER = H * DHX
    KI = INNER // P
    HALF = INNER // 2
    VX = DHX + 1
    with Stage(core, "x0") as s:
        SCALE = float(DHX) ** -0.5
        C = s.sb("C", [P, NB, D])
        wq, wk, wv = (s.sb(n, [P, KD, INNER]) for n in ("wq", "wk", "wv"))
        wo = s.sb("wo", [P, KI, D])
        gin, bin_ = (s.sb(n, [P, 2 * KD]) for n in ("gin", "bin"))
        gqk, bqk = (s.sb(n, [P, 2, KI]) for n in ("gqk", "bqk"))
        bot = s.sb("bot", [P, D])
        st = s.sb("st", [P, 2, 6])
        mvl, vel, rstdl = s.sb("mvl", [P, 2]), s.sb("vel", [P, 1]), s.sb("rstdl", [P, 1])
        xl = s.sb("xl", [P, 2, D])
        xlT = s.sb("xlT", [P, 2 * KD, P])
        qkn = s.sb("qkn", [P, 2, INNER])
        qkT = s.sb("qkT", [P, 2, KI, P])
        V = s.sb("V", [P, H, VX])
        mx = s.sb("mx", [P, 2, 2, 3])
        Sb, Pr, PTs = (s.sb(n, [P, 2, 2, 3, P]) for n in ("Sb", "Pr", "PTs"))
        rinv = s.sb("rinv", [P, 2, H // 2])
        on = s.sb("on", [P, INNER])
        oT = s.sb("oT", [P, KI, P])
        pB, pS, pT, pO = (s.ps(n, [P, 2, 512]) for n in ("pB", "pS", "pT", "pO"))
        y = pB[:, 0, 0:D]
        tail = Tail(s, core, pT[:, 0, 0:D].rearrange("p (k n) -> p k n", k=KD))

        LOADED = 16 * 14
        loaded = s.sem("loaded")
        ones_set = s.sem("ones_set")
        ln_var = s.sem("ln_var")
        ln_rstd = s.sem("ln_rstd")
        xl_ready = s.sem("xl_ready")
        t_ready = s.sem("t_ready")
        t_used = s.sem("t_used", 1)
        b_ready = s.sem("b_ready")
        b_used = s.sem("b_used", 1)
        qkn_ready = s.sem("qkn_ready")
        s_ready = s.sem("s_ready")
        s_used = s.sem("s_used", 1)
        p_ready = s.sem("p_ready")
        o_ready = s.sem("o_ready")
        o_norm = s.sem("o_norm", 1)
        vsteps = s.sem("vector_steps")
        block = s.block()
        TU, BU = 6, 3

        @block.sync
        def _(sp):
            sp.dma_start(C[:], a["ctx_1024"].rearrange("b t d -> t b d")).then_inc(loaded, 16)
            for dst, src in ((wq, "L0_xattn_Wq"), (wk, "L0_xattn_Wk"), (wv, "L0_xattn_Wv"), (wo, "L0_xattn_Wo")):
                sp.dma_start(dst[:], a[src].rearrange("(k p) n -> p k n", p=P)).then_inc(loaded, 16)
            sp.dma_start(bot[:], a["L0_xattn_bo"].partition_broadcast(P)).then_inc(loaded, 16)
            for dst, src in ((gin[:, 0:KD], "vid_g"), (gin[:, KD:], "tab_g"), (bin_[:, 0:KD], "vid_b"),
                             (bin_[:, KD:], "tab_b"), (gqk[:, 0, :], "q_g"), (gqk[:, 1, :], "k_g"),
                             (bqk[:, 0, :], "q_b"), (bqk[:, 1, :], "k_b")):
                sp.dma_start(dst, a[f"L0_xattn_{src}_cols"]).then_inc(loaded, 16)
            sp.wait_ge(loaded, LOADED)

        @block.gpsimd
        def _(pool):
            s.prime(pool)
            pool.memset(V[:], 1.0).then_inc(ones_set, 1)
            pool.wait_ge(loaded, LOADED)
            with pool.Fori(0, NB) as b:
                for i in range(4):
                    pool.wait_ge(ln_var, 4 * b + i + 1)
                    pool.tensor_tensor(rstdl[:], vel[:], core.mhalf[:], ALU.pow).then_inc(ln_rstd, 1)
                tail.pool_residual(pool, b, bot[:])
                tail.pool(pool, b)

        @block.tensor
        def _(pe):
            pe.wait_ge(loaded, LOADED)
            pe.wait_ge(ones_set, 1)
            with pe.Fori(0, NB) as b:
                pe.wait_ge(xl_ready, 2 * b + 2)
                pe.wait_ge(t_used, TU * b + 1)
                pe.wait_ge(tail.xT_stored, b + 1)
                for i in range(2):
                    for k in range(KD):
                        ins = pe.transpose(pT[:, 0, bass.ts(KD * i + k, P)], xl[:, i, bass.ts(k, P)], core.ident[:])
                ins.then_inc(t_ready, 1)
                pe.wait_ge(t_used, TU * b + 2)
                for i, (w, src) in enumerate(((wq, 0), (wv, KD), (wk, KD))):
                    pe.wait_ge(b_used, BU * b + i + 1)
                    if i == 0:
                        pe.wait_ge(tail.y_used, b + 1)
                    for n in range(2):
                        for k in range(KD):
                            ins = pe.matmul(pB[:, n, 0:HALF], xlT[:, src + k, :], w[:, k, bass.ts(n, HALF)],
                                            start=(k == 0), stop=(k == KD - 1))
                    ins.then_inc(b_ready, 1)
                for i in range(2):
                    pe.wait_ge(qkn_ready, 2 * b + i + 1)
                    pe.wait_ge(t_used, TU * b + 2 + i)
                    for k in range(KI):
                        ins = pe.transpose(pT[:, k // 3, bass.ts(k % 3, P)], qkn[:, i, bass.ts(k, P)], core.ident[:])
                    ins.then_inc(t_ready, 1)
                pe.wait_ge(t_used, TU * b + 4)
                for hf in range(2):
                    pe.wait_ge(s_used, 2 * b + hf + 1)
                    for c in range(3):
                        for j in range(2):
                            r = slice(DHX * j, DHX * (j + 1))
                            ins = pe.matmul(pS[:, j, bass.ts(c, P)], qkT[r, 0, 3 * hf + c, :], qkT[r, 1, 3 * hf + c, :],
                                            start=True, stop=True)
                    ins.then_inc(s_ready, 1)
                for hf in range(2):
                    pe.wait_ge(p_ready, 2 * b + hf + 1)
                    pe.wait_ge(t_used, TU * b + 4 + hf)
                    for j in range(2):
                        for c in range(3):
                            ins = pe.transpose(pT[:, j, bass.ts(c, P)], Pr[:, hf, j, c, :], core.ident[:])
                    ins.then_inc(t_ready, 1)
                pe.wait_ge(b_used, BU * b + 4)
                pe.wait_ge(o_norm, b + 1)
                for hf in range(2):
                    pe.wait_ge(t_used, TU * b + 5 + hf)
                    for j in range(2):
                        for c in range(3):
                            h = 2 * (3 * hf + c) + j
                            o = h % (H // 2) * VX
                            ins = pe.matmul(pO[:, h // (H // 2), o:o + VX], PTs[:, hf, j, c, :], V[:, h, :],
                                            start=True, stop=True)
                ins.then_inc(o_ready, 1)
                pe.wait_ge(o_norm, b + 2)
                for k in range(KI):
                    ins = pe.transpose(pT[:, k // 3, bass.ts(k % 3, P)], on[:, bass.ts(k, P)], core.ident[:])
                ins.then_inc(t_ready, 1)
                pe.wait_ge(t_used, TU * b + 7)
                for k in range(KI):
                    ins = pe.matmul(y, oT[:, k, :], wo[:, k, :], start=(k == 0), stop=(k == KI - 1))
                ins.then_inc(tail.y_ready, 1)
                tail.tensor(pe, b)

        def split(t):
            return t[:, :, 0:HALF].rearrange("p a (c n) -> p a c n", c=3)

        @block.scalar
        def _(act):
            act.wait_ge(loaded, LOADED)
            act.wait_ge(ones_set, 1)
            with act.Fori(0, NB) as b:
                act.wait_ge(t_ready, TU * b + 1)
                for k in range(2 * KD):
                    ins = act.activation(xlT[:, k, :], pT[:, 0, bass.ts(k, P)], ACT.Identity,
                                         bias=bin_[:, k:k + 1], scale=gin[:, k:k + 1])
                ins.then_inc(t_used, 1)
                act.wait_ge(b_ready, BU * b + 2)
                for n in range(2):
                    ins = act.copy(V[:, bass.ts(n, H // 2), 0:DHX],
                                   pB[:, n, 0:HALF].rearrange("p (h d) -> p h d", d=DHX))
                ins.then_inc(b_used, 1)
                for i in range(2):
                    act.wait_ge(t_ready, TU * b + 2 + i)
                    for k in range(KI):
                        ins = act.activation(qkT[:, i, k, :], pT[:, k // 3, bass.ts(k % 3, P)], ACT.Identity,
                                             bias=bqk[:, i, k:k + 1], scale=gqk[:, i, k:k + 1])
                    ins.then_inc(t_used, 1)
                for hf in range(2):
                    act.wait_ge(s_used, 2 * b + hf + 2)
                    act.activation(Pr[:, hf, :, :, :], Sb[:, hf, :, :, :], ACT.Exp, scale=SCALE).then_inc(p_ready, 1)
                for hf in range(2):
                    act.wait_ge(t_ready, TU * b + 4 + hf)
                    act.copy(PTs[:, hf, :, :, :], split(pT)).then_inc(t_used, 1)
                act.wait_ge(t_ready, TU * b + 6)
                act.copy(oT[:].rearrange("p (a c) n -> p a c n", a=2), split(pT)).then_inc(t_used, 1)
                tail.scalar(act, b)

        @block.vector
        def _(dve):
            dve.wait_ge(loaded, LOADED)
            steps = Steps(dve, vsteps, 4 * 2 + 2 + 1 + tail.STEPS)

            def moments(b, i, parts):
                for n, part in enumerate(parts):
                    if n < len(parts) - 1:
                        dve.bn_stats(st[:, n, :], part)
                    else:
                        steps.then(dve.bn_stats(st[:, n, :], part))
                hold(dve, core)
                steps.then(dve.bn_aggr(mvl[:], st[:, 0:len(parts), :].rearrange("p a n -> p (a n)")))
                dve.tensor_scalar(vel[:], mvl[:, 1:2], LN_EPS, None, ALU.add).then_inc(ln_var, 1)
                dve.wait_ge(ln_rstd, 4 * b + i + 1)

            with dve.Fori(0, NB) as b:
                steps.turn(b)
                for i, src in enumerate((core.X, C)):
                    moments(b, i, [src[:, b, :]])
                    hold(dve, core)
                    ins = dve.tensor_scalar(xl[:, i, :], src[:, b, :], mvl[:, 0:1], rstdl[:], ALU.subtract, ALU.mult)
                    ins.then_inc(xl_ready, 1)
                    dve.wait_ge(xl_ready, 2 * b + i + 1)
                for i in range(2):
                    dve.wait_ge(b_ready, BU * b + (1 if i == 0 else 3))
                    moments(b, 2 + i, [pB[:, 0, 0:HALF], pB[:, 1, 0:HALF]])
                    dve.tensor_scalar(qkn[:, i, :].rearrange("p (a n) -> p a n", a=2), pB[:, :, 0:HALF], mvl[:, 0:1],
                                      rstdl[:], ALU.subtract, ALU.mult).then_inc(qkn_ready, 1)
                    dve.wait_ge(qkn_ready, 2 * b + i + 1)
                    dve.sem_inc(b_used, 1)
                for hf in range(2):
                    dve.wait_ge(s_ready, 2 * b + hf + 1)
                    steps.then(dve.tensor_reduce(mx[:, hf, :, :], split(pS), AX.X, ALU.max))
                    for j in range(2):
                        ins = dve.tensor_tensor(Sb[:, hf, j, :, :], pS[:, j, 0:HALF].rearrange("p (c n) -> p c n", c=3),
                                                mx[:, hf, j, :].unsqueeze(2).to_broadcast([P, 3, P]), ALU.subtract)
                    ins.then_inc(s_used, 1)
                dve.wait_ge(o_ready, b + 1)
                ov = pO[:, :, 0:H // 2 * VX].rearrange("p a (h d) -> p a h d", d=VX)
                steps.then(dve.reciprocal(rinv[:], ov[:, :, :, DHX]))
                for j in range(2):
                    ins = dve.tensor_tensor(on[:, bass.ts(j, HALF)].rearrange("p (h d) -> p h d", d=DHX), ov[:, j, :, 0:DHX],
                                            rinv[:, j, :].unsqueeze(2).to_broadcast([P, H // 2, DHX]), ALU.mult)
                ins.then_inc(o_norm, 1)
                tail.vector(dve, steps, b, y)
                steps.end()


MAGIC = 12582912.0


def ternary(dve, steps, w, out, below, low, high):
    steps.then(dve.tensor_scalar(below, w, low, None, ALU.is_lt))
    steps.then(dve.scalar_tensor_tensor(out=out, in0=w, scalar=high, in1=below, op0=ALU.is_gt, op1=ALU.subtract))


def l0_ffn(core, a):
    F = 1024
    KF = F // P
    with ExitStack() as keep:
        wgb, wub, wdb = (keep.enter_context(core.nc.sbuf_tensor(n, [P, KD * F], BF16)) for n in ("wgb", "wub", "wdb"))
        m127 = keep.enter_context(core.nc.sbuf_tensor("m127", [P, 3], F32))
        identb = keep.enter_context(core.nc.sbuf_tensor("identb", [P, P], BF16))
        with Stage(core, "q0") as s:
            w32 = [s.sb(f"w{i}", [P, KD * F]) for i in range(3)]
            below = s.sb("below", [P, KD * F])
            sums, mean, low, high = (s.sb(n, [P, 3]) for n in ("sums", "mean", "low", "high"))
            pt = s.ps("pt", [P, 3])
            loaded = [s.sem(f"loaded{i}") for i in range(3)]
            summed = s.sem("summed")
            total = s.sem("total")
            chain = s.sem("vector_steps")
            block = s.block()

            @block.sync
            def _(sp):
                for i, (name, k) in enumerate((("L0_ffn_w_gateT", KD), ("L0_ffn_w_upT", KD), ("L0_ffn_w_downT", KF))):
                    sp.dma_start(w32[i][:].rearrange("p (k n) -> p k n", k=k),
                                 a[name].rearrange("(k p) n -> p k n", p=P)).then_inc(loaded[i], 16)
                for i in range(3):
                    sp.wait_ge(loaded[i], 16)

            @block.tensor
            def _(pe):
                pe.wait_ge(summed, 3)
                pe.matmul(pt[:], core.ones[:], sums[:], start=True, stop=True).then_inc(total, 1)

            @block.vector
            def _(dve):
                steps = Steps(dve, chain, 1000)
                steps.turn(0)
                for i in range(3):
                    dve.wait_ge(loaded[i], 16)
                    dve.tensor_reduce(sums[:, i:i + 1], w32[i][:], AX.X, ALU.add,
                                      apply_absolute_value=True).then_inc(summed, 1)
                dve.wait_ge(total, 1)
                steps.then(dve.tensor_scalar(mean[:], pt[:], 1.0 / (D * F), 1e-5, ALU.mult, ALU.max))
                steps.then(dve.tensor_scalar(low[:], mean[:], -0.5, None, ALU.mult))
                steps.then(dve.tensor_scalar(high[:], mean[:], 0.5, None, ALU.mult))
                steps.then(dve.tensor_scalar(m127[:], mean[:], 1.0 / 127.0, None, ALU.mult))
                steps.then(dve.tensor_copy(identb[:], core.ident[:]))
                for i, out in enumerate((wgb, wub, wdb)):
                    ternary(dve, steps, w32[i][:], out[:], below[:], low[:, i:i + 1], high[:, i:i + 1])

        l0_ffn_tokens(core, F, KF, wgb, wub, wdb, m127, identb)


def l0_ffn_tokens(core, F, KF, wgb, wub, wdb, m127, identb):
    N = F // 512
    with Stage(core, "f0") as s:
        xr = s.sb("xr", [P, D])
        xq = s.sb("xq", [P, D], BF16)
        xqT = s.sb("xqT", [P, KD, P], BF16)
        am, inv, sg, su = (s.sb(n, [P, 1]) for n in ("am", "inv", "sg", "su"))
        am2, inv2, sd = (s.sb(n, [P, 1]) for n in ("am2", "inv2", "sd"))
        gate, h = s.sb("gate", [P, F]), s.sb("h", [P, F])
        hq = s.sb("hq", [P, F], BF16)
        hqT = s.sb("hqT", [P, KF, P], BF16)
        pG, pU = s.ps("pG", [P, F]), s.ps("pU", [P, F])
        pt = s.ps("pt", [P, KD, P], BF16)
        pT = s.ps("pT", [P, KF, P], BF16)
        y = s.ps("y", [P, D])
        pX = s.ps("pX", [P, KD, P])
        tail = Tail(s, core, pX)
        xq_ready = s.sem("xq_ready")
        xqT_ready = s.sem("xqT_ready", 1)
        xqT_stored = s.sem("xqT_stored", 1)
        gu_ready = s.sem("gu_ready", 1)
        gate_ready = s.sem("gate_ready", 1)
        h_ready = s.sem("h_ready", 1)
        hq_ready = s.sem("hq_ready")
        hqT_ready = s.sem("hqT_ready", 1)
        hqT_stored = s.sem("hqT_stored", 1)
        vsteps = s.sem("vector_steps")
        block = s.block()

        @block.gpsimd
        def _(pool):
            s.prime(pool)
            with pool.Fori(0, NB) as b:
                tail.pool_residual(pool, b)
                tail.pool(pool, b)

        @block.tensor
        def _(pe):
            with pe.Fori(0, NB) as b:
                pe.wait_ge(xq_ready, b + 1)
                pe.wait_ge(xqT_stored, b + 1)
                for k in range(KD):
                    ins = pe.transpose(pt[:, k, :], xq[:, bass.ts(k, P)], identb[:])
                ins.then_inc(xqT_ready, 1)
                pe.wait_ge(xqT_stored, b + 2)
                pe.wait_ge(gate_ready, b + 1)
                pe.wait_ge(h_ready, b + 1)
                for w, out in ((wgb, pG), (wub, pU)):
                    for n in range(N):
                        for k in range(KD):
                            ins = pe.matmul(out[:, bass.ts(n, 512)], xqT[:, k, :],
                                            w[:, k * F + n * 512:k * F + (n + 1) * 512],
                                            start=(k == 0), stop=(k == KD - 1))
                ins.then_inc(gu_ready, 1)
                pe.wait_ge(hq_ready, b + 1)
                pe.wait_ge(hqT_stored, b + 1)
                for k in range(KF):
                    ins = pe.transpose(pT[:, k, :], hq[:, bass.ts(k, P)], identb[:])
                ins.then_inc(hqT_ready, 1)
                pe.wait_ge(hqT_stored, b + 2)
                pe.wait_ge(tail.y_used, b + 1)
                for k in range(KF):
                    ins = pe.matmul(y[:], hqT[:, k, :], wdb[:, bass.ts(k, D)], start=(k == 0), stop=(k == KF - 1))
                ins.then_inc(tail.y_ready, 1)
                tail.tensor(pe, b)

        @block.scalar
        def _(act):
            with act.Fori(0, NB) as b:
                act.wait_ge(xqT_ready, b + 2)
                act.wait_ge(gu_ready, b + 1)
                act.copy(xqT[:], pt[:]).then_inc(xqT_stored, 1)
                act.wait_ge(gu_ready, b + 2)
                act.wait_ge(h_ready, b + 1)
                act.activation(gate[:], pG[:], ACT.Silu, scale=sg[:]).then_inc(gate_ready, 1)
                act.wait_ge(hqT_ready, b + 2)
                act.copy(hqT[:], pT[:]).then_inc(hqT_stored, 1)
                tail.scalar(act, b)

        @block.vector
        def _(dve):
            steps = Steps(dve, vsteps, 13 + tail.STEPS)
            with dve.Fori(0, NB) as b:
                steps.turn(b)
                hold(dve, core)
                steps.then(dve.tensor_reduce(am[:], core.X[:, b, :], AX.X, ALU.max, apply_absolute_value=True))
                steps.then(dve.tensor_scalar(am[:], am[:], 1e-5, None, ALU.max))
                dve.wait_ge(gate_ready, b + 1)
                steps.then(dve.reciprocal(inv[:], am[:]))
                steps.then(dve.tensor_scalar(sg[:], am[:], m127[:, 0:1], None, ALU.mult))
                steps.then(dve.tensor_scalar(su[:], am[:], m127[:, 1:2], None, ALU.mult))
                steps.then(dve.tensor_scalar(inv[:], inv[:], 127.0, None, ALU.mult))
                hold(dve, core)
                steps.then(dve.tensor_scalar(xr[:], core.X[:, b, :], inv[:], MAGIC, ALU.mult, ALU.add))
                dve.wait_ge(xqT_ready, b + 1)
                dve.tensor_scalar(xq[:], xr[:], MAGIC, 127.0, ALU.subtract, ALU.min).then_inc(xq_ready, 1)
                dve.wait_ge(gate_ready, b + 2)
                dve.scalar_tensor_tensor(out=h[:], in0=pU[:], scalar=su[:], in1=gate[:], op0=ALU.mult,
                                         op1=ALU.mult).then_inc(h_ready, 1)
                dve.wait_ge(h_ready, b + 2)
                steps.then(dve.tensor_reduce(am2[:], h[:], AX.X, ALU.max, apply_absolute_value=True))
                steps.then(dve.tensor_scalar(am2[:], am2[:], 1e-5, None, ALU.max))
                steps.then(dve.reciprocal(inv2[:], am2[:]))
                steps.then(dve.tensor_scalar(inv2[:], inv2[:], 127.0, None, ALU.mult))
                steps.then(dve.tensor_scalar(sd[:], am2[:], m127[:, 2:3], None, ALU.mult))
                steps.then(dve.tensor_scalar(h[:], h[:], inv2[:], MAGIC, ALU.mult, ALU.add))
                dve.wait_ge(hqT_ready, b + 1)
                dve.tensor_scalar(hq[:], h[:], MAGIC, 127.0, ALU.subtract, ALU.min).then_inc(hq_ready, 1)
                tail.vector(dve, steps, b, y[:], scale=sd[:])
                steps.end()


def l1_attn(core, a):
    DI = 512
    KI = DI // P
    NX = 16 + D + DI
    TAPS = 4
    PAD = TAPS - 1
    with ExitStack() as keep:
        def sb(name, shape):
            return keep.enter_context(core.nc.sbuf_tensor(name, shape, F32))

        w_in, w_x, w_out = sb("w_in", [P, KD, DI]), sb("w_x", [P, KI, DI]), sb("w_out", [P, KI, D])
        mean = sb("means", [P, 3])
        with Stage(core, "q1") as s:
            raw = [s.sb("raw_in", [P, KD, 2 * DI]), s.sb("raw_x", [P, KI, NX]), s.sb("raw_out", [P, KI, D])]
            below = s.sb("below", [P, KI, DI])
            sums, low, high = (s.sb(n, [P, 3]) for n in ("sums", "low", "high"))
            pt = s.ps("pt", [P, 3])
            loaded = [s.sem(f"loaded{i}") for i in range(3)]
            summed, total, chain = s.sem("summed"), s.sem("total"), s.sem("vector_steps")
            block = s.block()

            @block.sync
            def _(sp):
                for i, name in enumerate(("L1_attn_w_inT", "L1_attn_w_xT", "L1_attn_w_outT")):
                    sp.dma_start(raw[i][:], a[name].rearrange("(k p) n -> p k n", p=P)).then_inc(loaded[i], 16)
                for i in range(3):
                    sp.wait_ge(loaded[i], 16)

            @block.tensor
            def _(pe):
                pe.wait_ge(summed, 3)
                pe.matmul(pt[:], core.ones[:], sums[:], start=True, stop=True).then_inc(total, 1)

            @block.vector
            def _(dve):
                steps = Steps(dve, chain, 1000)
                steps.turn(0)
                for i in range(3):
                    dve.wait_ge(loaded[i], 16)
                    dve.tensor_reduce(sums[:, i:i + 1], raw[i][:].rearrange("p k n -> p (k n)"), AX.X, ALU.add,
                                      apply_absolute_value=True).then_inc(summed, 1)
                dve.wait_ge(total, 1)
                for i, count in enumerate((D * 2 * DI, DI * NX, DI * D)):
                    steps.then(dve.tensor_scalar(mean[:, i:i + 1], pt[:, i:i + 1], 1.0 / count, LN_EPS, ALU.mult, ALU.max))
                steps.then(dve.tensor_scalar(low[:], mean[:], -0.5, None, ALU.mult))
                steps.then(dve.tensor_scalar(high[:], mean[:], 0.5, None, ALU.mult))
                ternary(dve, steps, raw[0][:, :, 0:DI], w_in[:], below[:, 0:KD, :], low[:, 0:1], high[:, 0:1])
                ternary(dve, steps, raw[1][:, :, 0:DI], w_x[:], below[:], low[:, 1:2], high[:, 1:2])
                ternary(dve, steps, raw[2][:], w_out[:], below[:, :, 0:D], low[:, 2:3], high[:, 2:3])

        with Stage(core, "a1") as s:
            b_in, b_conv, b_x = (s.sb(n, [P, KI]) for n in ("b_in", "b_conv", "b_x"))
            w_conv = s.sb("w_conv", [P, KI, TAPS])
            b_out = s.sb("b_out", [P, D])
            xi = s.sb("xi", [P, KI, G, PAD + P])
            cv = s.sb("cv", [P, 2, G, P])
            xc, gt, yT = (s.sb(n, [P, KI, GT]) for n in ("xc", "gt", "yT"))
            pA = [s.ps(f"pA{i}", [P, GT]) for i in range(2)]
            pD = [s.ps(f"pD{i}", [P, GT]) for i in range(2)]
            y = s.ps("y", [P, D])
            pX = s.ps("pX", [P, KD, P])
            tail = Tail(s, core, pX)
            LOADED = 16 * 5
            loaded = s.sem("loaded")
            zeroed = s.sem("zeroed")
            in_ready = s.sem("in_ready")
            in_stored = s.sem("in_stored", 2)
            conv_ready = s.sem("conv_ready", 1)
            xc_ready = s.sem("xc_ready", 2)
            d_ready = s.sem("d_ready")
            gate_ready = s.sem("gate_ready", 2)
            yT_ready = s.sem("yT_ready", 1)
            vsteps = s.sem("vector_steps")
            csteps = s.sem("conv_steps")
            block = s.block()

            @block.sync
            def _(sp):
                for dst, src in ((b_in[:], "b_in_cols"), (b_conv[:], "b_conv_cols"), (b_x[:], "b_x_cols"),
                                 (w_conv[:], "w_conv_cols")):
                    sp.dma_start(dst, a[f"L1_attn_{src}"]).then_inc(loaded, 16)
                sp.dma_start(b_out[:], a["L1_attn_b_out"].partition_broadcast(P)).then_inc(loaded, 16)
                sp.wait_ge(loaded, LOADED)

            @block.gpsimd
            def _(pool):
                s.prime(pool)
                pool.memset(xi[:], 0.0).then_inc(zeroed, 1)
                pool.wait_ge(loaded, LOADED)
                with pool.Fori(0, NB) as b:
                    tail.pool_residual(pool, b, b_out[:])
                    tail.pool(pool, b)

            @block.tensor
            def _(pe):
                with pe.Fori(0, NG) as g:
                    for m in range(KI):
                        pe.wait_ge(in_stored, KI * g + m + 1)
                        for k in range(KD):
                            ins = pe.matmul(pA[m % 2][:], w_in[:, k, bass.ts(m, P)], core.XT[:, k, bass.ts(g, GT)],
                                            start=(k == 0), stop=(k == KD - 1))
                        ins.then_inc(in_ready, 1)
                    pe.wait_ge(xc_ready, KI * g + KI + 2)
                    for m in range(KI):
                        pe.wait_ge(gate_ready, KI * g + m + 1)
                        for k in range(KI):
                            ins = pe.matmul(pD[m % 2][:], w_x[:, k, bass.ts(m, P)], xc[:, k, :],
                                            start=(k == 0), stop=(k == KI - 1))
                        ins.then_inc(d_ready, 1)
                    pe.wait_ge(yT_ready, g + 2)
                    for q in range(G):
                        b = G * g + q
                        pe.wait_ge(tail.y_used, b + 1)
                        for k in range(KI):
                            ins = pe.matmul(y[:], yT[:, k, bass.ts(q, P)], w_out[:, k, :],
                                            start=(k == 0), stop=(k == KI - 1))
                        ins.then_inc(tail.y_ready, 1)
                        tail.tensor(pe, b)

            @block.scalar
            def _(act):
                act.wait_ge(loaded, LOADED)
                act.wait_ge(zeroed, 1)
                with act.Fori(0, NG) as g:
                    for m in range(KI):
                        act.wait_ge(in_ready, KI * g + m + 1)
                        act.wait_ge(conv_ready, KI * g + 1)
                        act.activation(xi[:, m, :, PAD:], pA[m % 2][:].rearrange("p (s t) -> p s t", s=G), ACT.Identity,
                                       bias=b_in[:, m:m + 1], scale=mean[:, 0:1]).then_inc(in_stored, 1)
                    for m in range(KI):
                        act.wait_ge(conv_ready, KI * g + m + 2)
                        act.wait_ge(yT_ready, g + 1)
                        act.activation(xc[:, m, :], cv[:, m % 2, :, :].rearrange("p s t -> p (s t)"), ACT.Silu,
                                       bias=b_conv[:, m:m + 1]).then_inc(xc_ready, 1)
                    for m in range(KI):
                        act.wait_ge(d_ready, KI * g + m + 1)
                        act.activation(gt[:, m, :], pD[m % 2][:], ACT.Sigmoid, bias=b_x[:, m:m + 1],
                                       scale=mean[:, 1:2]).then_inc(gate_ready, 1)
                    for q in range(G):
                        tail.scalar(act, G * g + q)

            @block.vector
            def _(dve):
                dve.wait_ge(loaded, LOADED)
                csteps_ = Steps(dve, csteps, KI * (TAPS - 1))
                steps = Steps(dve, vsteps, tail.STEPS)
                with dve.Fori(0, NG) as g:
                    csteps_.turn(g)
                    for m in range(KI):
                        dve.wait_ge(in_stored, KI * g + m + 3)
                        dve.wait_ge(xc_ready, KI * g + m + 1)
                        c = cv[:, m % 2, :, :]
                        csteps_.then(dve.tensor_scalar(c, xi[:, m, :, 0:P], w_conv[:, m, 0:1], None, ALU.mult))
                        for j in range(1, TAPS):
                            ins = dve.scalar_tensor_tensor(out=c, in0=xi[:, m, :, j:j + P], scalar=w_conv[:, m, j:j + 1],
                                                           in1=c, op0=ALU.mult, op1=ALU.add)
                            if j < TAPS - 1:
                                csteps_.then(ins)
                        ins.then_inc(conv_ready, 1)
                    csteps_.end()
                    dve.wait_ge(gate_ready, KI * g + KI + 2)
                    dve.tensor_tensor(yT[:], xc[:], gt[:], ALU.mult).then_inc(yT_ready, 1)
                    for q in range(G):
                        b = G * g + q
                        steps.turn(b)
                        tail.vector(dve, steps, b, y[:], scale=mean[:, 2:3])
                        steps.end()


H16 = 16
DH = D // H16
NQT = 4
HH = H16 // NQT
HT = P // DH
VA = DH + 1


def attention16(core, a, name, Wq, Wk, Wv, Wo=None, bq=None, bk=None, bv=None, bo=None,
                own=False, rope=False, bias=None):
    with Stage(core, name) as s:
        SCALE = float(DH) ** -0.5
        KV = core.XT if own else core.CT
        moved = bq is not None

        wq, wk = (s.sb(n, [P, KD, D]) for n in ("wq", "wk"))
        wv = s.sb("wv", [P, KD, D])
        loads = [(wq, Wq), (wk, Wk), (wv, Wv)]
        if Wo:
            wo = s.sb("wo", [P, KD, D])
            loads.append((wo, Wo))
        if rope:
            wq2, wk2 = (s.sb(n, [P, KD, D]) for n in ("wq2", "wk2"))
            loads += [(wq2, Wq + "_partner"), (wk2, Wk + "_partner")]
        small = []
        if moved:
            bqc, bkc = (s.sb(n, [P, KD]) for n in ("bqc", "bkc"))
            small += [(bqc, bq), (bkc, bk)]
        if rope:
            bqc2, bkc2 = (s.sb(n, [P, KD]) for n in ("bqc2", "bkc2"))
            small += [(bqc2, bq + "_partner"), (bkc2, bk + "_partner")]
            cosT, sinT = (s.sb(n, [P, P]) for n in ("cosT", "sinT"))
            small += [(cosT, "c_cos"), (sinT, "c_sin")]
            turned_bias = [s.sb(n, [P, KD, P]) for n in ("bqT", "bkT")]
            tmpb = s.sb("tmpb", [P, KD, P])
        if bv:
            bvt = s.sb("bvt", [P, D])
        if bo:
            bot = s.sb("bot", [P, D])
        kvs = s.sb("kvs", [P, KD, P])
        qT = s.sb("qT", [P, KD, P])
        kx = s.sb("kx", [P, KD, HT, P])
        if rope:
            r1, r2 = (s.sb(n, [P, KD, P]) for n in ("r1", "r2"))
        own_head = s.sb("own_head", [P, HT])
        small.append((own_head, "c_own_head"))
        V = s.sb("V", [P, H16, VA])
        Sb = s.sb("Sb", [P, NQT, HH, P])
        if bias is not None:
            Ba = s.sb("Ba", [P, 2, HH, P])
        mx = s.sb("mx", [P, NQT, HH])
        Pr = s.sb("Pr", [P, NQT, HH, P])
        PTs = s.sb("PTs", [P, NQT, HH, P])
        rinv = s.sb("rinv", [P, H16])
        on = s.sb("on", [P, D])
        oT = s.sb("oT", [P, KD, P])

        pS = [s.ps(f"pS{i}", [P, HH, P]) for i in range(2)]
        pT = [s.ps(f"pT{i}", [P, HH, P]) for i in range(2)]
        pqk = s.ps("pqk", [P, 4, P])
        pvy = s.ps("pvy", [P, 2, D])
        pO = s.ps("pO", [P, H16, VA])
        pX = s.ps("pX", [P, 4, P])
        tail = Tail(s, core, pX[:, 2:4, :])

        LOADED = 16 * (len(loads) + len(small) + bool(bv) + bool(bo))
        loaded = s.sem("loaded")
        ones_set = s.sem("ones_set")
        tables = s.sem("tables")
        kv_staged = s.sem("kv_staged")
        qk_ready = s.sem("qk_ready")
        qk_used = s.sem("qk_used", 1)
        v_ready = s.sem("v_ready", 1)
        v_stored = s.sem("v_stored", 1)
        q_stored, k_stored = s.sem("q_stored"), s.sem("k_stored")
        s_ready = s.sem("s_ready", NQT)
        s_used = s.sem("s_used", 2)
        p_ready = s.sem("p_ready", NQT)
        pT_ready = s.sem("pT_ready", NQT)
        pT_stored = s.sem("pT_stored", 2)
        o_ready = s.sem("o_ready", 1)
        o_used = s.sem("o_used", 1)
        oT_ready = s.sem("oT_ready", 1)
        oT_stored = s.sem("oT_stored", 1)
        vsteps = s.sem("vector_steps")
        biased = s.sem("biased")
        project_steps, tail_steps = s.sem("project_steps"), s.sem("tail_steps")
        block = s.block()

        @block.sync
        def _(sp):
            for dst, src in loads:
                sp.dma_start(dst[:], a[src].rearrange("(k p) n -> p k n", p=P)).then_inc(loaded, 16)
            for dst, src in small:
                sp.dma_start(dst[:], a[src]).then_inc(loaded, 16)
            if bv:
                sp.dma_start(bvt[:], a[bv].partition_broadcast(P)).then_inc(loaded, 16)
            if bo:
                sp.dma_start(bot[:], a[bo].partition_broadcast(P)).then_inc(loaded, 16)
            sp.wait_ge(loaded, LOADED)

        @block.gpsimd
        def _(pool):
            s.prime(pool)
            pool.memset(V[:], 1.0).then_inc(ones_set, 1)
            pool.wait_ge(loaded, LOADED)

            def stage_kv(b):
                pool.wait_ge(v_ready, b + 1)
                hold(pool, core)
                pool.tensor_copy(kvs[:], KV[:, :, bass.ts(b, P)]).then_inc(kv_staged, 1)

            def rest(b):
                tail.pool_residual(pool, b, bot[:] if bo else None)
                tail.pool(pool, b)

            stage_kv(0)
            stage_kv(1)
            with pool.Fori(1, NB - 1) as n:
                stage_kv(n + 1)
                rest(n - 1)
            rest(NB - 2)
            rest(NB - 1)

        q_weights, k_weights = ((wq, wq2), (wk, wk2)) if rope else ((wq,), (wk,))

        @block.tensor
        def _(pe):
            pe.wait_ge(loaded, LOADED)

            def through_pqk(b, i, ws, src):
                pe.wait_ge(qk_used, 2 * b + i + 1)
                for t in range(KD * len(ws)):
                    for k in range(KD):
                        ins = pe.matmul(pqk[:, t, :], ws[t // KD][:, k, bass.ts(t % KD, P)], src[:, k, bass.ts(b, P)],
                                        start=(k == 0), stop=(k == KD - 1))
                ins.then_inc(qk_ready, 1)

            def scores(b, pair):
                if pair == 0:
                    pe.wait_ge(q_stored, b + 1)
                    pe.wait_ge(k_stored, b + 1)
                for qd in (2 * pair, 2 * pair + 1):
                    pe.wait_ge(s_used, NQT * b + qd + 1)
                    t, h = qd // 2, HH * (qd % 2)
                    pe.matmul(pS[qd % 2][:], qT[:, t, :], kx[:, t, h:h + HH, :], start=True, stop=True).then_inc(s_ready, 1)

            def turn_out(b):
                pe.wait_ge(o_used, b + 2)
                pe.wait_ge(oT_stored, b + 1)
                pe.wait_ge(tail.xT_stored, b + 1)
                for k in range(KD):
                    ins = pe.transpose(pX[:, k, :], on[:, bass.ts(k, P)], core.ident[:])
                ins.then_inc(oT_ready, 1)

            def value(b):
                pe.wait_ge(kv_staged, b + 1)
                pe.wait_ge(v_stored, b + 1)
                for k in range(KD):
                    ins = pe.matmul(pvy[:, 0, :], kvs[:, k, :], wv[:, k, :], start=(k == 0), stop=(k == KD - 1))
                ins.then_inc(v_ready, 1)

            def project_out(b):
                pe.wait_ge(oT_stored, b + 2)
                pe.wait_ge(tail.y_used, b + 1)
                for k in range(KD):
                    ins = pe.matmul(pvy[:, 1, :], oT[:, k, :], wo[:, k, :], start=(k == 0), stop=(k == KD - 1))
                ins.then_inc(tail.y_ready, 1)

            def turn(n, before=True, after=True):
                scores(n, 0)
                if before and Wo:
                    turn_out(n - 1)
                if after:
                    through_pqk(n + 1, 0, q_weights, core.XT)
                scores(n, 1)
                if after:
                    if before and Wo:
                        pe.wait_ge(tail.y_used, n)
                    value(n + 1)
                if before and Wo:
                    project_out(n - 1)
                if after:
                    through_pqk(n + 1, 1, k_weights, KV)
                products(n)
                if before:
                    tail.tensor(pe, n - 1)

            def products(b):
                def transposed(qd):
                    pe.wait_ge(p_ready, NQT * b + qd + NQT + 1)
                    pe.wait_ge(pT_stored, NQT * b + qd + 1)
                    for i in range(HH):
                        ins = pe.transpose(pT[qd % 2][:, i, :], Pr[:, qd, i, :], core.ident[:])
                    ins.then_inc(pT_ready, 1)

                def times_v(qd):
                    pe.wait_ge(pT_stored, NQT * b + qd + 3)
                    for i in range(HH):
                        head = HH * qd + i
                        ins = pe.matmul(pO[:, head, :], PTs[:, qd, i, :], V[:, head, :], start=True, stop=True)
                    return ins

                transposed(0)
                transposed(1)
                pe.wait_ge(v_stored, b + 2)
                pe.wait_ge(o_used, b + 1)
                times_v(0)
                transposed(2)
                times_v(1)
                transposed(3)
                times_v(2)
                times_v(3).then_inc(o_ready, 1)

            through_pqk(0, 0, q_weights, core.XT)
            value(0)
            through_pqk(0, 1, k_weights, KV)
            turn(0, before=False)
            with pe.Fori(1, NB - 1) as n:
                turn(n)
            turn(NB - 1, after=False)
            if Wo:
                turn_out(NB - 1)
                project_out(NB - 1)
            tail.tensor(pe, NB - 1)

        @block.scalar
        def _(act):
            act.wait_ge(loaded, LOADED)
            act.wait_ge(ones_set, 1)

            def query(b):
                act.wait_ge(qk_ready, 2 * b + 1)
                act.wait_ge(s_ready, NQT * b + NQT)
                if moved:
                    for t in range(KD):
                        ins = act.activation(qT[:, t, :], pqk[:, t, :], ACT.Identity, bias=bqc[:, t:t + 1])
                else:
                    ins = act.copy(qT[:], pqk[:, 0:KD, :])
                ins.then_inc(q_stored, 1)
                act.wait_ge(q_stored, b + 1)
                act.sem_inc(qk_used, 1)

            def value(b, after_y=False):
                if not bv:
                    act.wait_ge(v_ready, b + 2)
                    act.wait_ge(o_ready, b + 1)
                    if after_y:
                        act.wait_ge(tail.y_used, b)
                    act.copy(V[:, :, 0:DH], pvy[:, 0, :].rearrange("p (h d) -> p h d", d=DH)).then_inc(v_stored, 1)

            def exponentials(b, qd):
                act.wait_ge(s_used, NQT * b + qd + 3)
                act.wait_ge(pT_ready, NQT * b + qd + 1)
                act.activation(Pr[:, qd, :, :], Sb[:, qd, :, :], ACT.Exp, scale=SCALE).then_inc(p_ready, 1)

            def turn_out(b):
                if Wo:
                    act.wait_ge(oT_ready, b + 2)
                    act.copy(oT[:], pX[:, 0:2, :]).then_inc(oT_stored, 1)

            def turn(n, before=True, after=True):
                if before:
                    turn_out(n - 1)
                for qd in range(NQT):
                    exponentials(n, qd)
                    if after and not rope and qd == 1:
                        query(n + 1)
                act.wait_ge(o_ready, n + 1)
                for qd in range(NQT):
                    act.wait_ge(pT_ready, NQT * n + qd + NQT + 1)
                    act.copy(PTs[:, qd, :, :], pT[qd % 2][:]).then_inc(pT_stored, 1)
                if after:
                    value(n + 1, after_y=before)
                if before:
                    tail.scalar(act, n - 1)

            if not rope:
                query(0)
            value(0)
            turn(0, before=False)
            with act.Fori(1, NB - 1) as n:
                turn(n)
            turn(NB - 1, after=False)
            turn_out(NB - 1)
            tail.scalar(act, NB - 1)

        @block.vector
        def _(dve):
            dve.wait_ge(loaded, LOADED)
            dve.wait_ge(ones_set, 1)
            if rope:
                for i, (c, c2) in enumerate(((bqc, bqc2), (bkc, bkc2))):
                    dve.tensor_tensor(turned_bias[i][:], c[:].unsqueeze(2).to_broadcast([P, KD, P]),
                                      cosT[:].unsqueeze(1).to_broadcast([P, KD, P]), ALU.mult).then_inc(tables, 1)
                    dve.tensor_tensor(tmpb[:], c2[:].unsqueeze(2).to_broadcast([P, KD, P]),
                                      sinT[:].unsqueeze(1).to_broadcast([P, KD, P]), ALU.mult).then_inc(tables, 1)
                    dve.wait_ge(tables, 3 * i + 2)
                    dve.tensor_tensor(turned_bias[i][:], turned_bias[i][:], tmpb[:], ALU.add).then_inc(tables, 1)
                    dve.wait_ge(tables, 3 * i + 3)
            steps = Steps(dve, vsteps, 2 + NQT * (1 if bias is None else 2))
            psteps = Steps(dve, project_steps, 5)
            tsteps = Steps(dve, tail_steps, tail.STEPS)

            def value(b):
                dve.wait_ge(v_ready, b + 2)
                dve.wait_ge(o_ready, b + 1)
                dve.tensor_tensor(V[:, :, 0:DH], pvy[:, 0, :].rearrange("p (h d) -> p h d", d=DH),
                                  bvt[:].rearrange("p (h d) -> p h d", d=DH), ALU.add).then_inc(v_stored, 1)

            def expand(src, b):
                for t in range(KD):
                    wide = src[:, t, :].unsqueeze(1).to_broadcast([P, HT, P])
                    mask = own_head[:].unsqueeze(2).to_broadcast([P, HT, P])
                    if moved and not rope:
                        ins = dve.scalar_tensor_tensor(out=kx[:, t, :, :], in0=wide, scalar=bkc[:, t:t + 1], in1=mask,
                                                       op0=ALU.add, op1=ALU.mult)
                    else:
                        ins = dve.tensor_tensor(kx[:, t, :, :], wide, mask, ALU.mult)
                ins.then_inc(k_stored, 1)

            def turned(b, i, out):
                dve.wait_ge(qk_ready, 2 * b + i + 1)
                both = [P, KD, P]
                psteps.then(dve.tensor_tensor(r1[:], pqk[:, 0:KD, :], cosT[:].unsqueeze(1).to_broadcast(both), ALU.mult))
                psteps.then(dve.tensor_tensor(r2[:], pqk[:, KD:, :], sinT[:].unsqueeze(1).to_broadcast(both), ALU.mult))
                dve.sem_inc(qk_used, 1)
                dve.tensor_tensor(r1[:], r1[:], turned_bias[i][:], ALU.add).then_inc(biased, 1)
                dve.wait_ge(biased, 2 * b + i + 1)
                return dve.tensor_tensor(out, r1[:], r2[:], ALU.add)

            def projections(b):
                psteps.turn(b)
                if rope:
                    dve.wait_ge(s_ready, NQT * b + NQT)
                    turned(b, 0, qT[:]).then_inc(q_stored, 1)
                    dve.wait_ge(q_stored, b + 1)
                    hold(dve, core)
                    psteps.then(turned(b, 1, r1[:]))
                    expand(r1, b)
                else:
                    dve.wait_ge(qk_ready, 2 * b + 2)
                    dve.wait_ge(s_ready, NQT * b + NQT)
                    expand(pqk, b)
                    dve.wait_ge(k_stored, b + 1)
                    dve.sem_inc(qk_used, 1)

            def shifted(b):
                steps.turn(b)
                for qd in range(NQT):
                    dve.wait_ge(s_ready, NQT * b + qd + NQT + 1)
                    src = pS[qd % 2][:]
                    if bias is not None:
                        hold(dve, core)
                        steps.then(dve.tensor_tensor(Ba[:, qd % 2, :, :], src,
                                                     bias[:, b, :].unsqueeze(1).to_broadcast([P, HH, P]), ALU.add))
                        src = Ba[:, qd % 2, :, :]
                    steps.then(dve.tensor_reduce(mx[:, qd, :], src, AX.X, ALU.max))
                    dve.wait_ge(p_ready, NQT * b + qd + 1)
                    dve.tensor_tensor(Sb[:, qd, :, :], src, mx[:, qd, :].unsqueeze(2).to_broadcast([P, HH, P]),
                                      ALU.subtract).then_inc(s_used, 1)

            def normalise(b):
                dve.wait_ge(o_ready, b + 2)
                steps.then(dve.reciprocal(rinv[:], pO[:, :, DH]))
                dve.wait_ge(oT_ready, b + 1) if Wo else dve.wait_ge(tail.xn_ready, b + 1)
                steps.then(dve.tensor_tensor(on[:].rearrange("p (h d) -> p h d", d=DH), pO[:, :, 0:DH],
                                             rinv[:].unsqueeze(2).to_broadcast([P, H16, DH]), ALU.mult))
                dve.sem_inc(o_used, 1)

            def finish(b):
                tsteps.turn(b)
                if Wo:
                    tail.vector(dve, tsteps, b, pvy[:, 1, :])
                else:
                    dve.wait_ge(tail.xn_ready, b + 1)
                    dve.wait_ge(tail.xres_ready, b + 1)
                    tsteps.then(dve.tensor_tensor(tail.r[:], on[:], tail.xres[:], ALU.add))
                    tail.norm(dve, tsteps, b)
                tsteps.end()

            def turn(n, before=True, after=True):
                shifted(n)
                if after:
                    projections(n + 1)
                if before:
                    finish(n - 1)
                if after and bv:
                    dve.wait_ge(o_ready, n + 2)
                    value(n + 1)
                normalise(n)
                steps.end()

            projections(0)
            if bv:
                value(0)
            turn(0, before=False)
            with dve.Fori(1, NB - 1) as n:
                turn(n)
            turn(NB - 1, after=False)
            finish(NB - 1)


def l1_xattn(core, a):
    attention16(core, a, "x1", "L1_xattn_WqT", "L1_xattn_WkT", "L1_xattn_WvT", "L1_xattn_WoT",
                "L1_xattn_bq_cols", "L1_xattn_bk_cols", "L1_xattn_bv", "L1_xattn_bo", rope=True)


def l2_xattn(core, a):
    with core.nc.sbuf_tensor("mask_bias", [P, NB, P], F32) as bias:
        with Stage(core, "mask") as s:
            m = s.sb("m", [P, NB, P], I32)
            loaded = s.sem("loaded")
            block = s.block()

            @block.sync
            def _(sp):
                sp.dma_start(m[:], a["mask_BxSxS2_if1"].rearrange("b q k -> q b k")).then_inc(loaded, 16)
                sp.wait_ge(loaded, 16)

            @block.vector
            def _(dve):
                dve.wait_ge(loaded, 16)
                dve.tensor_scalar(bias[:], m[:], 0.0, MASKED, ALU.is_equal, ALU.mult)

        attention16(core, a, "x2", "L2_xattn_w_qT", "L2_xattn_w_kT", "L2_xattn_w_vT", "L2_xattn_w_oT",
                    bo="L2_xattn_b_o", bias=bias)


def l3_xattn(core, a):
    attention16(core, a, "x3", "L3_xattn_Wq", "L3_xattn_Wk", "L3_xattn_Wv", "L3_xattn_Wo",
                bo="L3_xattn_bo")


def l3_attn(core, a):
    with core.nc.sbuf_tensor("score_bias", [P, NB, P], F32) as bias:
        l3_penalties(core, a, bias)
        attention16(core, a, "a3", "L3_attn_Wq", "L3_attn_Wk", "L3_attn_Wv", None,
                    "L3_attn_bq_cols", "L3_attn_bk_cols", "L3_attn_bv", own=True, bias=bias)


def l3_penalties(core, a, bias):
    LIFT = 2.0 ** 53
    BASE = float(np.log(P - 2.0))
    with Stage(core, "pen") as s:
        wg = s.sb("wg", [P, KD, P])
        bgt = s.sb("bgt", [P, 1])
        dist = s.sb("dist", [P, P])
        wgc = s.sb("wgc", [P, KD])
        ej = s.sb("ej", [P, P])
        zj = s.sb("zj", [P, P])
        t1, t2, t3 = (s.sb(n, [P, P]) for n in ("t1", "t2", "t3"))
        zi, oz, sc = (s.sb(n, [P, 1]) for n in ("zi", "oz", "sc"))
        pj = s.ps("pj", [P, P])
        loaded = s.sem("loaded")
        g_ready = s.sem("g_ready")
        e_ready = s.sem("e_ready", 1)
        zi_ready = s.sem("zi_ready", 1)
        scope_ready = s.sem("scope_ready", 1)
        pen_ready = s.sem("pen_ready", 1)
        log_done = s.sem("log_done", 1)
        vs = s.sem("vector_steps")
        wide = s.sem("wide")
        block = s.block()

        @block.sync
        def _(sp):
            sp.dma_start(wgc[:], a["L3_attn_Wg_cols"]).then_inc(loaded, 16)
            sp.dma_start(bgt[:], a["L3_attn_bg"].partition_broadcast(P)).then_inc(loaded, 16)
            sp.dma_start(dist[:], a["c_dist"]).then_inc(loaded, 16)
            sp.wait_ge(loaded, 48)

        @block.gpsimd
        def _(pool):
            s.prime(pool)

        @block.tensor
        def _(pe):
            pe.wait_ge(wide, 1)
            with pe.Fori(0, NB) as b:
                pe.wait_ge(e_ready, b + 1)
                for k in range(KD):
                    ins = pe.matmul(pj[:], wg[:, k, :], core.XT[:, k, bass.ts(b, P)], start=(k == 0), stop=(k == KD - 1))
                ins.then_inc(g_ready, 1)

        @block.scalar
        def _(act):
            act.wait_ge(wide, 2)
            with act.Fori(0, NB) as b:
                act.wait_ge(g_ready, b + 1)
                act.wait_ge(zi_ready, b + 1)
                act.activation(ej[:], pj[:], ACT.Exp, bias=bgt[:], scale=-1.0).then_inc(e_ready, 1)
                act.wait_ge(zi_ready, b + 2)
                act.wait_ge(scope_ready, b + 1)
                act.activation(sc[:], oz[:], ACT.Exp, scale=BASE).then_inc(scope_ready, 1)
                act.wait_ge(pen_ready, b + 2)
                hold(act, core)
                act.activation(bias[:, b, :], t3[:], ACT.Ln, scale=LIFT).then_inc(log_done, 1)

        @block.vector
        def _(dve):
            dve.wait_ge(loaded, 48)
            dve.tensor_copy(wg[:], wgc[:].unsqueeze(2).to_broadcast([P, KD, P])).then_inc(wide, 1)
            dve.wait_ge(wide, 1)
            dve.tensor_scalar(bgt[:], bgt[:], -1.0, None, ALU.mult).then_inc(wide, 1)
            steps = Steps(dve, vs, 12)
            with dve.Fori(0, NB) as b:
                steps.turn(b)
                dve.wait_ge(e_ready, b + 2)
                dve.wait_ge(log_done, b + 1)
                steps.then(dve.tensor_scalar(ej[:], ej[:], 1.0, None, ALU.add))
                steps.then(dve.reciprocal(zj[:], ej[:]))
                steps.then(dve.tensor_tensor(t1[:], zj[:], core.ident[:], ALU.mult))
                steps.then(dve.tensor_reduce(zi[:], t1[:], AX.X, ALU.add))
                steps.then(dve.tensor_scalar(oz[:], zi[:], -1.0, 1.0, ALU.mult, ALU.add))
                dve.sem_inc(zi_ready, 1)
                steps.then(dve.tensor_scalar(t1[:], zj[:], -1.0, oz[:], ALU.mult, ALU.add))
                steps.then(dve.tensor_scalar(t1[:], t1[:], 0.0, oz[:], ALU.max, ALU.mult))
                steps.then(dve.tensor_scalar(t2[:], zj[:], oz[:], 1.0, ALU.add, ALU.min))
                steps.then(dve.scalar_tensor_tensor(out=t1[:], in0=t2[:], scalar=zi[:], in1=t1[:], op0=ALU.mult, op1=ALU.add))
                dve.wait_ge(scope_ready, b + 2)
                steps.then(dve.tensor_scalar(t3[:], dist[:], sc[:], 1.0, ALU.add, ALU.min))
                steps.then(dve.scalar_tensor_tensor(out=t3[:], in0=t3[:], scalar=1e-32, in1=t1[:], op0=ALU.max, op1=ALU.mult))
                steps.then(dve.tensor_scalar(t3[:], t3[:], 1e-32, None, ALU.max))
                dve.sem_inc(pen_ready, 1)
                steps.end()
            dve.wait_ge(log_done, NB + 1)
            dve.tensor_scalar(bias[:], bias[:], float(DH) ** 0.5, None, ALU.mult)


def l2_attn(core, a):
    H = 8
    with Stage(core, "a2") as s:
        SCALE = float(P) ** -0.5
        wq = s.sb("wq", [P, KD, H * P])
        wk, wv = (s.sb(n, [P, KD, P]) for n in ("wk", "wv"))
        wo = s.sb("wo", [P, H, D])
        peT, causal = (s.sb(n, [P, P]) for n in ("peT", "causal"))
        pe0 = s.sb("pe0", [P, 1])
        kvs = s.sb("kvs", [P, KD, P])
        qT, oT, Ba, Sb, Pr, PTs = (s.sb(n, [P, H, P]) for n in ("qT", "oT", "Ba", "Sb", "Pr", "PTs"))
        kT, V = (s.sb(n, [P, P]) for n in ("kT", "V"))
        mx, sm, rinv = (s.sb(n, [P, H]) for n in ("mx", "sm", "rinv"))
        pQ, pS, pT = (s.ps(n, [P, H, P]) for n in ("pQ", "pS", "pT"))
        pvy = s.ps("pvy", [P, 3, P])
        pX = s.ps("pX", [P, KD + 1, P])
        y = pvy[:, 1:3, :].rearrange("p a n -> p (a n)")
        tail = Tail(s, core, pX[:, 0:KD, :])

        LOADED = 16 * 7
        loaded = s.sem("loaded")
        kv_staged = s.sem("kv_staged")
        q_ready = s.sem("q_ready")
        k_ready = s.sem("k_ready")
        v_ready = s.sem("v_ready", 1)
        q_stored, k_stored = s.sem("q_stored", 1), s.sem("k_stored", 1)
        v_stored = s.sem("v_stored", 1)
        s_ready = s.sem("s_ready", 1)
        s_masked = s.sem("s_masked", 1)
        s_shifted = s.sem("s_shifted")
        e_ready = s.sem("e_ready", 1)
        p_ready = s.sem("p_ready")
        pT_ready = s.sem("pT_ready", 1)
        pT_stored = s.sem("pT_stored")
        o_ready = s.sem("o_ready", 1)
        o_stored = s.sem("o_stored", 1)
        vsteps = s.sem("vector_steps")
        block = s.block()

        @block.sync
        def _(sp):
            for dst, src in ((wq, "L2_attn_WqT"), (wk, "L2_attn_WkT"), (wv, "L2_attn_WvT"), (wo, "L2_attn_WoT")):
                sp.dma_start(dst[:], a[src].rearrange("(k p) n -> p k n", p=P)).then_inc(loaded, 16)
            for dst, src in ((peT, "c_peT"), (causal, "c_causal"), (pe0, "c_pe0")):
                sp.dma_start(dst[:], a[src]).then_inc(loaded, 16)
            sp.wait_ge(loaded, LOADED)

        @block.gpsimd
        def _(pool):
            s.prime(pool)

            def stage_kv(b):
                pool.wait_ge(v_ready, b + 1)
                hold(pool, core)
                pool.tensor_copy(kvs[:], core.XT[:, :, bass.ts(b, P)]).then_inc(kv_staged, 1)

            def rest(b):
                tail.pool_residual(pool, b)
                tail.pool(pool, b)

            stage_kv(0)
            with pool.Fori(0, NB - 1) as b:
                stage_kv(b + 1)
                rest(b)
            rest(NB - 1)

        @block.tensor
        def _(pe):
            pe.wait_ge(loaded, LOADED)

            def projections(b, first=False):
                pe.wait_ge(q_stored, b + 1)
                for h in range(H):
                    for k in range(KD):
                        ins = pe.matmul(pQ[:, h, :], wq[:, k, bass.ts(h, P)], core.XT[:, k, bass.ts(b, P)],
                                        start=(k == 0), stop=(k == KD - 1))
                ins.then_inc(q_ready, 1)
                pe.wait_ge(k_stored, b + 1)
                if not first:
                    pe.wait_ge(tail.xT_stored, b)
                for k in range(KD):
                    ins = pe.matmul(pX[:, KD, :], wk[:, k, :], core.XT[:, k, bass.ts(b, P)],
                                    start=(k == 0), stop=(k == KD - 1))
                ins.then_inc(k_ready, 1)
                pe.wait_ge(kv_staged, b + 1)
                pe.wait_ge(v_stored, b + 1)
                for k in range(KD):
                    ins = pe.matmul(pvy[:, 0, :], kvs[:, k, :], wv[:, k, :], start=(k == 0), stop=(k == KD - 1))
                ins.then_inc(v_ready, 1)

            def scores(b):
                pe.wait_ge(q_stored, b + 2)
                pe.wait_ge(k_stored, b + 2)
                pe.wait_ge(s_masked, b + 1)
                for h in range(H):
                    ins = pe.matmul(pS[:, h, :], qT[:, h, :], kT[:], start=True, stop=True)
                ins.then_inc(s_ready, 1)

            def rest(b):
                pe.wait_ge(p_ready, b + 1)
                pe.wait_ge(o_stored, b + 1)
                for h in range(H):
                    ins = pe.transpose(pT[:, h, :], Pr[:, h, :], core.ident[:])
                ins.then_inc(pT_ready, 1)
                pe.wait_ge(pT_stored, b + 1)
                pe.wait_ge(v_stored, b + 2)
                for i in range(2):
                    ins = pe.matmul(pT[:, bass.ts(i, H // 2), :], V[:], PTs[:, bass.ts(i, H // 2), :],
                                    start=True, stop=True)
                ins.then_inc(o_ready, 1)
                pe.wait_ge(o_stored, b + 2)
                pe.wait_ge(tail.y_used, b + 1)
                for h in range(H):
                    ins = pe.matmul(y, oT[:, h, :], wo[:, h, :], start=(h == 0), stop=(h == H - 1))
                ins.then_inc(tail.y_ready, 1)
                tail.tensor(pe, b)

            projections(0, first=True)
            with pe.Fori(0, NB - 1) as b:
                scores(b)
                projections(b + 1)
                rest(b)
            scores(NB - 1)
            rest(NB - 1)

        @block.scalar
        def _(act):
            def value(b):
                act.wait_ge(v_ready, b + 2)
                act.wait_ge(o_ready, b + 1)
                act.copy(V[:], pvy[:, 0, :]).then_inc(v_stored, 1)

            def rest(b, last=False):
                act.wait_ge(s_shifted, b + 1)
                act.wait_ge(pT_ready, b + 1)
                act.activation(Pr[:], Sb[:], ACT.Exp, scale=SCALE).then_inc(e_ready, 1)
                act.wait_ge(pT_ready, b + 2)
                act.wait_ge(o_ready, b + 1)
                act.copy(PTs[:], pT[:]).then_inc(pT_stored, 1)
                if not last:
                    value(b + 1)
                act.wait_ge(o_ready, b + 2)
                act.copy(oT[:], pT[:]).then_inc(o_stored, 1)
                tail.scalar(act, b)

            value(0)
            with act.Fori(0, NB - 1) as b:
                rest(b)
            rest(NB - 1, last=True)

        @block.vector
        def _(dve):
            dve.wait_ge(loaded, LOADED)
            steps = Steps(dve, vsteps, 4 + tail.STEPS)

            def projections(b):
                dve.wait_ge(q_ready, b + 1)
                dve.wait_ge(s_ready, b + 1)
                dve.tensor_tensor(qT[:], pQ[:], peT[:].unsqueeze(1).to_broadcast([P, H, P]), ALU.add).then_inc(q_stored, 1)
                dve.wait_ge(k_ready, b + 1)
                dve.tensor_scalar(kT[:], pX[:, KD, :], pe0[:], None, ALU.add).then_inc(k_stored, 1)

            def shifted(b):
                steps.turn(b)
                dve.wait_ge(s_ready, b + 2)
                steps.then(dve.tensor_tensor(Ba[:], pS[:], causal[:].unsqueeze(1).to_broadcast([P, H, P]), ALU.add))
                dve.sem_inc(s_masked, 1)
                steps.then(dve.tensor_reduce(mx[:], Ba[:], AX.X, ALU.max))
                dve.wait_ge(e_ready, b + 1)
                dve.tensor_tensor(Sb[:], Ba[:], mx[:].unsqueeze(2).to_broadcast([P, H, P]),
                                  ALU.subtract).then_inc(s_shifted, 1)

            def rest(b):
                dve.wait_ge(e_ready, b + 2)
                steps.then(dve.tensor_reduce(sm[:], Pr[:], AX.X, ALU.add))
                steps.then(dve.reciprocal(rinv[:], sm[:]))
                dve.tensor_tensor(Pr[:], Pr[:], rinv[:].unsqueeze(2).to_broadcast([P, H, P]),
                                  ALU.mult).then_inc(p_ready, 1)
                tail.vector(dve, steps, b, y)

            projections(0)
            with dve.Fori(0, NB - 1) as b:
                shifted(b)
                projections(b + 1)
                rest(b)
                steps.end()
            shifted(NB - 1)
            rest(NB - 1)


E8 = 8
FH = 1024
KH = FH // P


def route_logits(core, a, name, w_name, logits):
    with Stage(core, name) as s:
        w = s.sb("w", [P, KD, E8])
        xs = s.sb("xs", [P, KD, P])
        pl = s.ps("pl", [P, NB, E8])
        loaded = s.sem("loaded")
        staged = s.sem("staged")
        logit_ready = s.sem("logit_ready", 1)
        block = s.block()

        @block.sync
        def _(sp):
            sp.dma_start(w[:], a[w_name].rearrange("(k p) n -> p k n", p=P)).then_inc(loaded, 16)
            sp.wait_ge(loaded, 16)

        @block.gpsimd
        def _(pool):
            s.prime(pool)
            with pool.Fori(0, NB) as b:
                pool.wait_ge(logit_ready, b + 1)
                hold(pool, core)
                pool.tensor_copy(xs[:], core.XT[:, :, bass.ts(b, P)]).then_inc(staged, 1)

        @block.tensor
        def _(pe):
            pe.wait_ge(loaded, 16)
            with pe.Fori(0, NB) as b:
                pe.wait_ge(staged, b + 1)
                for k in range(KD):
                    ins = pe.matmul(pl[:, b, :], xs[:, k, :], w[:, k, :], start=(k == 0), stop=(k == KD - 1))
                ins.then_inc(logit_ready, 1)

        @block.vector
        def _(dve):
            dve.wait_ge(logit_ready, NB + 1)
            dve.tensor_copy(logits[:], pl[:])


def first_largest(dve, steps, t, m, eq, order):
    wide = [P, NB, E8]
    steps.then(dve.tensor_reduce(m[:], t[:], AX.X, ALU.max))
    steps.then(dve.tensor_tensor(eq[:], t[:], m[:].unsqueeze(2).to_broadcast(wide), ALU.is_equal))
    steps.then(dve.tensor_tensor(eq[:], eq[:], order[:].unsqueeze(1).to_broadcast(wide), ALU.mult))
    steps.then(dve.tensor_reduce(m[:], eq[:], AX.X, ALU.max))
    steps.then(dve.tensor_tensor(eq[:], eq[:], m[:].unsqueeze(2).to_broadcast(wide), ALU.is_equal))


def route_top(core, a, name, W, top, bias_name=None):
    wide = [P, NB, E8]
    with Stage(core, name) as s:
        m = s.sb("m", [P, NB])
        oh, oh2, t = (s.sb(n, wide) for n in ("oh", "oh2", "t"))
        order, bias = s.sb("order", [P, E8]), s.sb("bias", [P, E8])
        loaded, shifted, exped, chain = s.sem("loaded"), s.sem("shifted"), s.sem("exped"), s.sem("vector_steps")
        LOADED = 16 * (1 + bool(bias_name))
        block = s.block()

        @block.sync
        def _(sp):
            sp.dma_start(order[:], a["c_order"]).then_inc(loaded, 16)
            if bias_name:
                sp.dma_start(bias[:], a[bias_name].partition_broadcast(P)).then_inc(loaded, 16)
            sp.wait_ge(loaded, LOADED)

        @block.scalar
        def _(act):
            act.wait_ge(shifted, 1)
            act.activation(t[:], t[:], ACT.Exp).then_inc(exped, 1)

        @block.vector
        def _(dve):
            steps = Steps(dve, chain, 1000)
            steps.turn(0)
            dve.wait_ge(loaded, LOADED)
            if bias_name:
                steps.then(dve.tensor_tensor(W[:], W[:], bias[:].unsqueeze(1).to_broadcast(wide), ALU.add))
            steps.then(dve.tensor_reduce(m[:], W[:], AX.X, ALU.max))
            dve.tensor_tensor(t[:], W[:], m[:].unsqueeze(2).to_broadcast(wide), ALU.subtract).then_inc(shifted, 1)
            dve.wait_ge(exped, 1)
            steps.then(dve.tensor_reduce(m[:], t[:], AX.X, ALU.add))
            steps.then(dve.reciprocal(m[:], m[:]))
            steps.then(dve.tensor_tensor(W[:], t[:], m[:].unsqueeze(2).to_broadcast(wide), ALU.mult))
            if top == 0:
                return
            first_largest(dve, steps, W, m, oh, order)
            if top == 1:
                steps.then(dve.scalar_tensor_tensor(out=W[:], in0=W[:], scalar=2.0, in1=oh[:], op0=ALU.mult, op1=ALU.mult))
                steps.then(dve.memset(W[:, :, E8 - 1:E8], 1.0))
                return
            steps.then(dve.tensor_tensor(t[:], W[:], oh[:], ALU.mult))
            steps.then(dve.tensor_tensor(t[:], W[:], t[:], ALU.subtract))
            steps.then(dve.tensor_tensor(t[:], t[:], oh[:], ALU.subtract))
            first_largest(dve, steps, t, m, oh2, order)
            steps.then(dve.tensor_tensor(oh[:], oh[:], oh2[:], ALU.add))
            steps.then(dve.tensor_tensor(W[:], W[:], oh[:], ALU.mult))
            steps.then(dve.tensor_reduce(m[:], W[:], AX.X, ALU.add))
            steps.then(dve.tensor_scalar(m[:], m[:], 1e-6, None, ALU.add))
            steps.then(dve.reciprocal(m[:], m[:]))
            steps.then(dve.tensor_tensor(W[:], W[:], m[:].unsqueeze(2).to_broadcast(wide), ALU.mult))


def route_choice(core, a, name, W):
    KEEP = NB * P // E8
    wide = [P, NB, E8]
    with Stage(core, name) as s:
        thr, cand, bit = (s.sb(n, [P, E8], I32) for n in ("thr", "cand", "bit"))
        cmp_, gt, eq, pre = (s.sb(n, wide) for n in ("cmp", "gt", "eq", "pre"))
        cnt, need = s.sb("cnt", [P, E8]), s.sb("need", [P, E8])
        ok = s.sb("ok", [P, E8], I32)
        tri = s.sb("tri", [P, P])
        pc = s.ps("pc", [P, E8])
        pp, pq = s.ps("pp", wide), s.ps("pq", wide)
        loaded = s.sem("loaded")
        counted = s.sem("counted")
        summed = s.sem("summed")
        ranked = s.sem("ranked")
        chain, loop_steps = s.sem("vector_steps"), s.sem("search_steps")
        BITS = 30
        block = s.block()

        @block.sync
        def _(sp):
            sp.dma_start(tri[:], a["c_before"]).then_inc(loaded, 16)
            sp.wait_ge(loaded, 16)

        @block.tensor
        def _(pe):
            with pe.Fori(0, BITS) as i:
                pe.wait_ge(counted, i + 1)
                pe.matmul(pc[:], core.ones[:], cnt[:], start=True, stop=True).then_inc(summed, 1)
            pe.wait_ge(counted, BITS + 1)
            pe.matmul(pc[:], core.ones[:], cnt[:], start=True, stop=True).then_inc(summed, 1)
            pe.wait_ge(loaded, 16)
            pe.wait_ge(counted, BITS + 2)
            pe.matmul(pp[:].rearrange("p b e -> p (b e)"), tri[:], eq[:].rearrange("p b e -> p (b e)"),
                      start=True, stop=True)
            pe.matmul(pq[:].rearrange("p b e -> p (b e)"), core.ones[:], eq[:].rearrange("p b e -> p (b e)"),
                      start=True, stop=True).then_inc(ranked, 1)

        @block.vector
        def _(dve):
            first = Steps(dve, chain, 1000)
            first.turn(0)
            first.then(dve.memset(thr[:], 0))
            first.then(dve.memset(bit[:], 1 << (BITS - 1)))
            steps = Steps(dve, loop_steps, 7)
            byexpert = "p b e -> p e b"
            with dve.Fori(0, BITS) as i:
                steps.turn(i)
                steps.then(dve.tensor_tensor(cand[:], thr[:], bit[:], ALU.bitwise_or))
                steps.then(dve.tensor_tensor(cmp_[:], W[:], cand[:].bitcast(F32).unsqueeze(1).to_broadcast(wide), ALU.is_ge))
                dve.tensor_reduce(cnt[:], cmp_[:].rearrange(byexpert), AX.X, ALU.add).then_inc(counted, 1)
                dve.wait_ge(summed, i + 1)
                steps.then(dve.tensor_scalar(ok[:], pc[:], float(KEEP), None, ALU.is_ge))
                steps.then(dve.tensor_scalar(ok[:], ok[:], -1.0, None, ALU.mult))
                steps.then(dve.tensor_tensor(cand[:], bit[:], ok[:], ALU.bitwise_and))
                steps.then(dve.tensor_tensor(thr[:], thr[:], cand[:], ALU.bitwise_or))
                steps.then(dve.tensor_scalar(bit[:], bit[:], 1, None, ALU.logical_shift_right))
                steps.end()
            t = thr[:].bitcast(F32).unsqueeze(1).to_broadcast(wide)
            first.then(dve.tensor_tensor(gt[:], W[:], t, ALU.is_gt))
            first.then(dve.tensor_tensor(eq[:], W[:], t, ALU.is_equal))
            dve.tensor_reduce(cnt[:], gt[:].rearrange(byexpert), AX.X, ALU.add).then_inc(counted, 1)
            dve.wait_ge(summed, BITS + 1)
            dve.tensor_scalar(need[:], pc[:], -1.0, float(KEEP), ALU.mult, ALU.add).then_inc(counted, 1)
            dve.wait_ge(ranked, 1)
            first.then(dve.tensor_copy(pre[:], pp[:]))
            first.then(dve.memset(cmp_[:, 0, :], 0.0))
            for b in range(1, NB):
                first.then(dve.tensor_tensor(cmp_[:, b, :], cmp_[:, b - 1, :], pq[:, b - 1, :], ALU.add))
            first.then(dve.tensor_tensor(pre[:], pre[:], cmp_[:], ALU.add))
            first.then(dve.tensor_tensor(pre[:], pre[:], need[:].unsqueeze(1).to_broadcast(wide), ALU.is_lt))
            first.then(dve.tensor_tensor(eq[:], eq[:], pre[:], ALU.mult))
            first.then(dve.tensor_tensor(gt[:], gt[:], eq[:], ALU.add))
            first.then(dve.tensor_tensor(W[:], W[:], gt[:], ALU.mult))


def experts(core, a, name, W, acc, up, down, act_fn, gate=None, b1=None):
    U = 2
    with Stage(core, name) as s:
        wu = [s.sb(f"wu{i}", [P, KD, FH]) for i in range(2)]
        wg = [s.sb(f"wg{i}", [P, KD, FH]) for i in range(2)] if gate else None
        wd = [s.sb(f"wd{i}", [P, KH, D]) for i in range(2)]
        b1c = [s.sb(f"b1c{i}", [P, KH]) for i in range(2)] if b1 else None
        hT = [s.sb(f"hT{i}", [P, KH, GT]) for i in range(2)]
        sg = [s.sb(f"sg{i}", [P, GT]) for i in range(2)] if gate else None
        pU = [s.ps(f"pU{i}", [P, GT]) for i in range(2)]
        pG = [s.ps(f"pG{i}", [P, GT]) for i in range(2)] if gate else None
        pY = [s.ps(f"pY{i}", [P, D]) for i in range(2)]
        NL = 2 + bool(gate) + bool(b1)
        loaded = [s.sem(f"loaded{i}") for i in range(2)]
        used = s.sem("used", 2)
        zeroed = s.sem("zeroed")
        u_ready = s.sem("u_ready")
        g_done = s.sem("g_done", 2)
        h_done = s.sem("h_done", 2)
        y_ready = s.sem("y_ready", 2)
        y_used = s.sem("y_used", 2)
        block = s.block()

        def groups_before(i, eu, t, u):
            return (2 * i + eu) * NG + U * t + u

        @block.sync
        def _(sp):
            with sp.Fori(0, E8 // 2) as i:
                for eu in range(2):
                    e = 2 * i + eu
                    sp.wait_ge(used, e + 1)
                    hold(sp, core)
                    sp.dma_start(wu[eu][:], a[up][e].rearrange("(k p) n -> p k n", p=P)).then_inc(loaded[eu], 16)
                    if gate:
                        sp.dma_start(wg[eu][:], a[gate][e].rearrange("(k p) n -> p k n", p=P)).then_inc(loaded[eu], 16)
                    if b1:
                        sp.dma_start(b1c[eu][:], a[b1][e]).then_inc(loaded[eu], 16)
                    sp.dma_start(wd[eu][:], a[down][e].rearrange("(k p) n -> p k n", p=P)).then_inc(loaded[eu], 16)
            for eu in range(2):
                sp.wait_ge(loaded[eu], 16 * NL * E8 // 2)

        @block.gpsimd
        def _(pool):
            s.prime(pool)
            pool.memset(acc[:], 0.0).then_inc(zeroed, 1)

        @block.tensor
        def _(pe):
            with pe.Fori(0, E8 // 2) as i:
                for eu in range(2):
                    pe.wait_ge(loaded[eu], 16 * NL * (i + 1))
                    hold(pe, core)
                    with pe.Fori(0, NG // U) as t:
                        for u in range(U):
                            n = groups_before(i, eu, t, u)
                            x = core.XT[:, :, bass.ts(U * t + u, GT)]
                            for m in range(KH):
                                pe.wait_ge(h_done, KH * n + m + 1)
                                for k in range(KD):
                                    ins = pe.matmul(pU[m % 2][:], wu[eu][:, k, bass.ts(m, P)], x[:, k, :],
                                                    start=(k == 0), stop=(k == KD - 1))
                                if gate:
                                    for k in range(KD):
                                        ins = pe.matmul(pG[m % 2][:], wg[eu][:, k, bass.ts(m, P)], x[:, k, :],
                                                        start=(k == 0), stop=(k == KD - 1))
                                ins.then_inc(u_ready, 1)
                        for u in range(U):
                            n = groups_before(i, eu, t, u)
                            pe.wait_ge(h_done, KH * (n + 1) + 2)
                            for q in range(G):
                                pe.wait_ge(y_used, G * n + q + 1)
                                for k in range(KH):
                                    ins = pe.matmul(pY[q % 2][:], hT[u][:, k, bass.ts(q, P)], wd[eu][:, k, :],
                                                    start=(k == 0), stop=(k == KH - 1))
                                ins.then_inc(y_ready, 1)
                    pe.wait_ge(y_ready, G * NG * (2 * i + eu + 1) + 2)
                    pe.sem_inc(used, 1)

        @block.scalar
        def _(act):
            with act.Fori(0, E8 // 2) as i:
                for eu in range(2):
                    if b1:
                        act.wait_ge(loaded[eu], 16 * NL * (i + 1))
                        hold(act, core)
                    with act.Fori(0, NG // U) as t:
                        for u in range(U):
                            n = groups_before(i, eu, t, u)
                            if not gate:
                                act.wait_ge(y_ready, G * (n - u) + 2)
                            for m in range(KH):
                                act.wait_ge(u_ready, KH * n + m + 1)
                                if gate:
                                    act.wait_ge(h_done, KH * n + m + 1)
                                    act.activation(sg[m % 2][:], pG[m % 2][:], act_fn).then_inc(g_done, 1)
                                elif b1:
                                    act.activation(hT[u][:, m, :], pU[m % 2][:], act_fn,
                                                   bias=b1c[eu][:, m:m + 1]).then_inc(h_done, 1)
                                else:
                                    act.activation(hT[u][:, m, :], pU[m % 2][:], act_fn).then_inc(h_done, 1)

        @block.vector
        def _(dve):
            dve.wait_ge(zeroed, 1)
            with dve.Fori(0, E8 // 2) as i:
                for eu in range(2):
                    with dve.Fori(0, NG // U) as t:
                        if gate:
                            for u in range(U):
                                n = groups_before(i, eu, t, u)
                                dve.wait_ge(y_ready, G * (n - u) + 2)
                                for m in range(KH):
                                    dve.wait_ge(g_done, KH * n + m + 3)
                                    dve.tensor_tensor(hT[u][:, m, :], pU[m % 2][:], sg[m % 2][:],
                                                      ALU.mult).then_inc(h_done, 1)
                        for u in range(U):
                            n = groups_before(i, eu, t, u)
                            for q in range(G):
                                b = G * (U * t + u) + q
                                dve.wait_ge(y_ready, G * n + q + 3)
                                hold(dve, core)
                                dve.scalar_tensor_tensor(out=acc[:, b, :], in0=pY[q % 2][:], scalar=W[:, b, bass.ds(2 * i + eu, 1)],
                                                         in1=acc[:, b, :], op0=ALU.mult, op1=ALU.add).then_inc(y_used, 1)
                                dve.wait_ge(y_used, G * n + q + 3)
                                hold(dve, core)


def add_experts(core, a, name, acc, W, b2=None, own_norm=False):
    with Stage(core, name) as s:
        pX = s.ps("pX", [P, KD, P])
        tail = Tail(s, core, pX)
        if b2:
            b2s = s.sb("b2s", [E8, D])
            wT = s.sb("wT", [E8, P])
            ws = s.sb("ws", [P, E8])
            pw = s.ps("pw", [E8, P])
            y = s.ps("y", [P, D])
            w_staged = s.sem("w_staged")
            wT_ready = s.sem("wT_ready", 1)
            wT_stored = s.sem("wT_stored")
        loaded = s.sem("loaded")
        vsteps = s.sem("vector_steps")
        own_ve = s.sem("own_ve")
        own_rstd = s.sem("own_rstd")
        st, mv, ve, rstd, an = (s.sb(n, sh) for n, sh in (("st", [P, 6]), ("mv2", [P, 2]), ("ve2", [P, 1]), ("rstd2", [P, 1]), ("an", [P, D])))
        block = s.block()

        @block.sync
        def _(sp):
            if b2:
                sp.dma_start(b2s[:], a[b2]).then_inc(loaded, 16)
                sp.wait_ge(loaded, 16)

        @block.gpsimd
        def _(pool):
            s.prime(pool)
            with pool.Fori(0, NB) as b:
                if b2:
                    pool.wait_ge(wT_ready, b + 1)
                    hold(pool, core)
                    pool.tensor_copy(ws[:], W[:, b, :]).then_inc(w_staged, 1)
                if own_norm:
                    tail.pool_residual(pool, b)
                    pool.wait_ge(own_ve, b + 1)
                    pool.tensor_tensor(rstd[:], ve[:], core.mhalf[:], ALU.pow).then_inc(own_rstd, 1)
                else:
                    tail.pool_residual(pool, b, acc[:, b, :])
                tail.pool(pool, b)

        @block.tensor
        def _(pe):
            if b2:
                pe.wait_ge(loaded, 16)
            with pe.Fori(0, NB) as b:
                if b2:
                    pe.wait_ge(w_staged, b + 1)
                    pe.transpose(pw[:], ws[:], core.ident[:]).then_inc(wT_ready, 1)
                    pe.wait_ge(wT_stored, b + 1)
                    pe.wait_ge(tail.y_used, b + 1)
                    pe.matmul(y[:], wT[:], b2s[:], start=True, stop=True).then_inc(tail.y_ready, 1)
                tail.tensor(pe, b)

        @block.scalar
        def _(act):
            with act.Fori(0, NB) as b:
                if b2:
                    act.wait_ge(wT_ready, b + 2)
                    act.wait_ge(tail.y_used, b + 1)
                    act.copy(wT[:], pw[:]).then_inc(wT_stored, 1)
                tail.scalar(act, b)

        @block.vector
        def _(dve):
            steps = Steps(dve, vsteps, tail.STEPS + (3 if own_norm else 0))
            with dve.Fori(0, NB) as b:
                steps.turn(b)
                if own_norm:
                    hold(dve, core)
                    steps.then(dve.bn_stats(st[:], acc[:, b, :]))
                    hold(dve, core)
                    steps.then(dve.bn_aggr(mv[:], st[:]))
                    dve.tensor_scalar(ve[:], mv[:, 1:2], LN_EPS, None, ALU.add).then_inc(own_ve, 1)
                    dve.wait_ge(own_rstd, b + 1)
                    hold(dve, core)
                    steps.then(dve.tensor_scalar(an[:], acc[:, b, :], mv[:, 0:1], rstd[:], ALU.subtract, ALU.mult))
                if b2:
                    tail.vector(dve, steps, b, y[:])
                else:
                    dve.wait_ge(tail.xn_ready, b + 1)
                    dve.wait_ge(tail.xres_ready, b + 1)
                    if own_norm:
                        steps.then(dve.scalar_tensor_tensor(out=tail.r[:], in0=tail.xres[:], scalar=2.0, in1=an[:],
                                                            op0=ALU.mult, op1=ALU.add))
                    else:
                        steps.then(dve.tensor_copy(tail.r[:], tail.xres[:]))
                    tail.norm(dve, steps, b)
                steps.end()


def moe_buffers(core, keep, name):
    return (keep.enter_context(core.nc.sbuf_tensor(name + "_W", [P, NB, E8], F32)),
            keep.enter_context(core.nc.sbuf_tensor(name + "_acc", [P, NB, D], F32)))


def l1_ffn(core, a):
    with ExitStack() as keep:
        W, acc = moe_buffers(core, keep, "moe1")
        route_logits(core, a, "rl1", "L1_ffn_w_router", W)
        route_top(core, a, "rt1", W, 1)
        experts(core, a, "e1", W, acc, "L1_ffn_up8", "L1_ffn_down8", ACT.Silu, gate="L1_ffn_gate8")
        add_experts(core, a, "ae1", acc, W)


def l2_ffn(core, a):
    with ExitStack() as keep:
        W, acc = moe_buffers(core, keep, "moe2")
        route_logits(core, a, "rl2", "L2_ffn_Ws", W)
        route_top(core, a, "rt2", W, 0, "L2_ffn_bs")
        route_choice(core, a, "rc2", W)
        experts(core, a, "e2", W, acc, "L2_ffn_W1", "L2_ffn_W2", ACT.Gelu_apprx_tanh, b1="L2_ffn_b1_cols")
        add_experts(core, a, "ae2", acc, W, b2="L2_ffn_b2")


def l3_ffn(core, a):
    with ExitStack() as keep:
        W, acc = moe_buffers(core, keep, "moe3")
        route_logits(core, a, "rl3", "L3_ffn_gate_wT", W)
        route_top(core, a, "rt3", W, 2, "L3_ffn_expert_bias")
        experts(core, a, "e3", W, acc, "L3_ffn_w_upT", "L3_ffn_w_downT", ACT.Gelu)
        add_experts(core, a, "ae3", acc, W, own_norm=True)


def partner_columns():
    c = np.arange(D)
    half = DH // 2
    return c + np.where(c % DH < half, half, -half)


def constants():
    t = np.arange(P)
    half = DH // 2
    inv = 1.0 / 10000.0 ** (np.arange(0, DH, 2, dtype=np.float32) / DH)
    angle = np.outer(inv[np.arange(P) % half], 10.0 * (t / P)).astype(np.float32)
    sign = np.where(np.arange(P) % DH < half, -1.0, 1.0)[:, None]
    inv_pe = np.exp(-np.log(np.float32(10000.0)) * (np.arange(0, P, 2, dtype=np.float32) / P))
    ang = t[:, None].astype(np.float32) * inv_pe[None, :]
    pe = np.zeros((P, P), np.float32)
    pe[:, 0::2], pe[:, 1::2] = np.sin(ang), np.cos(ang)
    return {
        "c_peT": np.ascontiguousarray(pe.T),
        "c_pe0": np.ascontiguousarray(pe[0:1].T),
        "c_causal": np.where(t[:, None] >= t[None, :], 0.0, MASKED).astype(np.float32),
        "c_order": np.broadcast_to(8.0 - np.arange(8, dtype=np.float32), (P, 8)).copy(),
        "c_before": (t[:, None] < t[None, :]).astype(np.float32),
        "c_own_head": (np.arange(P)[:, None] // DH == np.arange(P // DH)[None, :]).astype(np.float32),
        "c_ident": np.eye(P, dtype=np.float32),
        "c_dist": (2.0 - np.abs(t[:, None] - t[None, :])).astype(np.float32),
        "c_cos": np.cos(angle).astype(np.float32),
        "c_sin": (sign * np.sin(angle)).astype(np.float32),
    }


STAGES = [l0_attn, l0_xattn, l0_ffn, l1_attn, l1_xattn, l1_ffn, l2_attn, l2_xattn, l2_ffn, l3_attn, l3_xattn, l3_ffn]


def build(nc, a, out):
    with ExitStack() as ctx:
        core = Core(nc, ctx)
        setup(core, a)
        for stage in STAGES:
            stage(core, a)
        store(core, out)


TRANSPOSED = ["L0_attn_W_u", "L0_attn_W_g", "L0_attn_Bm", "L0_attn_A", "L0_attn_Cm",
              "L1_xattn_Wq", "L1_xattn_Wk", "L1_xattn_Wv", "L1_xattn_Wo",
              "L2_xattn_w_q", "L2_xattn_w_k", "L2_xattn_w_v", "L2_xattn_w_o",
              "L2_attn_Wq", "L2_attn_Wk", "L2_attn_Wv", "L2_attn_Wo",
              "L0_ffn_w_gate", "L0_ffn_w_up", "L0_ffn_w_down", "L1_attn_w_in", "L1_attn_w_x", "L1_attn_w_out",
              "L3_ffn_gate_w", "L3_ffn_w_up", "L3_ffn_w_down"]
COLUMNS = ["L0_attn_b_u", "L0_attn_b_g", "L3_attn_Wg",
           "L0_xattn_tab_g", "L0_xattn_tab_b", "L0_xattn_vid_g", "L0_xattn_vid_b",
           "L0_xattn_q_g", "L0_xattn_q_b", "L0_xattn_k_g", "L0_xattn_k_b", "L1_attn_b_conv",
           "L1_xattn_bq", "L1_xattn_bk", "L3_attn_bq", "L3_attn_bk"]

def kernel(**inputs):
    import concourse.bacc as _bacc
    from concourse.bass_utils import run_bass_kernel_spmd as _run

    nc = _bacc.Bacc("TRN2", target_bir_lowering=False, num_devices=1)
    arrays = {}
    for name, value in inputs.items():
        arrays[name] = np.ascontiguousarray(value)
    arrays["xT"] = np.ascontiguousarray(inputs["x"].reshape(NB * P, D).T)
    arrays["ctxT"] = np.ascontiguousarray(inputs["ctx_1024"].reshape(NB * P, D).T)
    for name in TRANSPOSED:
        arrays[name + "T"] = np.ascontiguousarray(np.swapaxes(arrays[name], -1, -2))
    for name in COLUMNS:
        arrays[name + "_cols"] = np.ascontiguousarray(arrays[name].reshape(-1, P).T)
    for name in ("L1_xattn_Wq", "L1_xattn_Wk"):
        arrays[name + "T_partner"] = np.ascontiguousarray(arrays[name + "T"][:, partner_columns()])
    for name in ("L1_xattn_bq", "L1_xattn_bk"):
        arrays[name + "_cols_partner"] = np.ascontiguousarray(arrays[name][partner_columns()].reshape(-1, P).T)
    arrays["L1_attn_b_in_cols"] = np.ascontiguousarray(arrays["L1_attn_b_in"][:4 * P].reshape(-1, P).T)
    arrays["L1_attn_b_x_cols"] = np.ascontiguousarray(arrays["L1_attn_b_x"][:4 * P].reshape(-1, P).T)
    arrays["L1_attn_w_conv_cols"] = np.ascontiguousarray(arrays["L1_attn_w_conv"].reshape(-1, P, 4).transpose(1, 0, 2))
    arrays["L2_ffn_b1_cols"] = np.ascontiguousarray(arrays["L2_ffn_b1"].reshape(8, -1, P).transpose(0, 2, 1))
    for part in ("up", "gate", "down"):
        arrays[f"L1_ffn_{part}8"] = np.concatenate([arrays[f"L1_ffn_w_{part}"], arrays[f"L1_ffn_ws_{part}"][None]])
    arrays.update(constants())
    a = {name: nc.dram_tensor(f"in_{name}", v.shape, mybir.dt.from_np(v.dtype), kind="ExternalInput").ap()
         for name, v in arrays.items()}
    out = nc.dram_tensor("out_x", (NB, P, D), F32, kind="ExternalOutput").ap()
    build(nc, a, out)
    r = _run(nc, [{f"in_{name}": v for name, v in arrays.items()}], core_ids=[0])
    return r.results[0]["out_x"]
```
